# Optimizing a Trainium2 kernel written in Bass

```python
import numpy as np
import jax
import jax.numpy as jnp

def _softmax(x, axis=-1):
    return jax.nn.softmax(x, axis=axis)
def _gelu(x):
    return jax.nn.gelu(x, approximate=True)
def _silu(x):
    return jax.nn.silu(x)
def _sigmoid(x):
    return jax.nn.sigmoid(x)
def _layernorm(x, axis=-1, eps=1e-5):
    m = jnp.mean(x, axis=axis, keepdims=True)
    v = jnp.var(x, axis=axis, keepdims=True)
    return (x - m) / jnp.sqrt(v + eps)
def _scatter_add(tgt, idx, src, axis=0):
    return tgt.at[idx].add(src)
def _segment_sum(src, seg, n):
    return jax.ops.segment_sum(src, seg, n)

kernel_name = 'mk_conv_seq_d1_conv_nchw256_40551f'

def setup_inputs(seed: int = 0):
    np.random.seed(seed)
    _w = jnp.asarray
    def _rec_inputs():
        import jax
        import jax.numpy as jnp
        _gk = jax.random.key(seed)
        x = -9.26e-05 + 0.9999 * jax.random.normal(jax.random.fold_in(_gk, 1), (16, 256, 96, 96), jnp.float32)
        return x
    x = _rec_inputs()
    def _L0_conv_setup():
        import jax, jax.numpy as jnp
        import numpy as np
        B, C, H, W = (16, 256, 96, 96)
        P = 16
        G = 8
        EPS = 1e-05

        def _forward(x, prototypes, pos_embed, q_w, q_b, k_w, k_b, v_w, v_b, out_w, out_b, dw_w, bn_g, bn_b, bn_mean, bn_var, gn_g, gn_b):
            b, c, h, w = x.shape
            residual = x
            pos = jax.image.resize(pos_embed, (1, c, h, w), method='bilinear')
            xp = x + pos
            q = jnp.einsum('bchw,dc->bhwd', xp, q_w) + q_b
            q = q.reshape(b, h * w, c)
            k = prototypes[0] @ k_w.T + k_b
            v = prototypes[0] @ v_w.T + v_b
            scale = c ** (-0.5)
            attn = jax.nn.softmax(jnp.einsum('bnc,pc->bnp', q, k) * scale, axis=-1)
            out = jnp.einsum('bnp,pc->bnc', attn, v)
            out = out.reshape(b, h, w, c).transpose(0, 3, 1, 2)
            out = jnp.einsum('bchw,dc->bdhw', out, out_w) + out_b[None, :, None, None]
            dw = jax.lax.conv_general_dilated(out, dw_w, window_strides=(1, 1), padding='SAME', feature_group_count=c, dimension_numbers=('NCHW', 'OIHW', 'NCHW'))
            inv = (bn_g / jnp.sqrt(bn_var + EPS))[None, :, None, None]
            bn = (dw - bn_mean[None, :, None, None]) * inv + bn_b[None, :, None, None]
            out = out + jax.nn.gelu(bn, approximate=False)
            y = out + residual
            yg = y.reshape(b, G, c // G, h, w)
            mu = yg.mean(axis=(2, 3, 4), keepdims=True)
            var = yg.var(axis=(2, 3, 4), keepdims=True)
            yn = ((yg - mu) * jax.lax.rsqrt(var + EPS)).reshape(b, c, h, w)
            return yn * gn_g[None, :, None, None] + gn_b[None, :, None, None]
        key = jax.random.key(seed)
        ks = jax.random.split(key, 18)
        n = jax.random.normal
        return {'x': n(ks[0], (B, C, H, W), jnp.float32), 'prototypes': n(ks[1], (1, P, C), jnp.float32), 'pos_embed': n(ks[2], (1, C, 64, 64), jnp.float32) * 0.02, 'q_w': n(ks[3], (C, C), jnp.float32) * C ** (-0.5), 'q_b': n(ks[4], (C,), jnp.float32) * 0.01, 'k_w': n(ks[5], (C, C), jnp.float32) * C ** (-0.5), 'k_b': n(ks[6], (C,), jnp.float32) * 0.01, 'v_w': n(ks[7], (C, C), jnp.float32) * C ** (-0.5), 'v_b': n(ks[8], (C,), jnp.float32) * 0.01, 'out_w': n(ks[9], (C, C), jnp.float32) * C ** (-0.5), 'out_b': n(ks[10], (C,), jnp.float32) * 0.01, 'dw_w': n(ks[11], (C, 1, 3, 3), jnp.float32) * (1.0 / 3.0), 'bn_g': 1.0 + 0.1 * n(ks[12], (C,), jnp.float32), 'bn_b': 0.1 * n(ks[13], (C,), jnp.float32), 'bn_mean': 0.05 * n(ks[14], (C,), jnp.float32), 'bn_var': 0.5 + jax.random.uniform(ks[15], (C,), jnp.float32), 'gn_g': 1.0 + 0.1 * n(ks[16], (C,), jnp.float32), 'gn_b': 0.1 * n(ks[17], (C,), jnp.float32)}
    _L0_conv_all = _L0_conv_setup()
    _L0_conv_in = {k: v for k, v in _L0_conv_all.items() if k in ('prototypes', 'pos_embed', 'q_w', 'q_b', 'k_w', 'k_b', 'v_w', 'v_b', 'out_w', 'out_b', 'dw_w', 'bn_g', 'bn_b', 'bn_mean', 'bn_var', 'gn_g', 'gn_b', )}
    del _L0_conv_all

    return {
        "x": x,
        "L0_conv_prototypes": _L0_conv_in["prototypes"],
        "L0_conv_pos_embed": _L0_conv_in["pos_embed"],
        "L0_conv_q_w": _L0_conv_in["q_w"],
        "L0_conv_q_b": _L0_conv_in["q_b"],
        "L0_conv_k_w": _L0_conv_in["k_w"],
        "L0_conv_k_b": _L0_conv_in["k_b"],
        "L0_conv_v_w": _L0_conv_in["v_w"],
        "L0_conv_v_b": _L0_conv_in["v_b"],
        "L0_conv_out_w": _L0_conv_in["out_w"],
        "L0_conv_out_b": _L0_conv_in["out_b"],
        "L0_conv_dw_w": _L0_conv_in["dw_w"],
        "L0_conv_bn_g": _L0_conv_in["bn_g"],
        "L0_conv_bn_b": _L0_conv_in["bn_b"],
        "L0_conv_bn_mean": _L0_conv_in["bn_mean"],
        "L0_conv_bn_var": _L0_conv_in["bn_var"],
        "L0_conv_gn_g": _L0_conv_in["gn_g"],
        "L0_conv_gn_b": _L0_conv_in["gn_b"],
    }

def reference(x, L0_conv_prototypes, L0_conv_pos_embed, L0_conv_q_w, L0_conv_q_b, L0_conv_k_w, L0_conv_k_b, L0_conv_v_w, L0_conv_v_b, L0_conv_out_w, L0_conv_out_b, L0_conv_dw_w, L0_conv_bn_g, L0_conv_bn_b, L0_conv_bn_mean, L0_conv_bn_var, L0_conv_gn_g, L0_conv_gn_b):
    import jax
    import jax.numpy as jnp
    def _L0_conv_ref(x, prototypes, pos_embed, q_w, q_b, k_w, k_b, v_w, v_b, out_w, out_b, dw_w, bn_g, bn_b, bn_mean, bn_var, gn_g, gn_b):
        import jax, jax.numpy as jnp
        import numpy as np
        B, C, H, W = (16, 256, 96, 96)
        P = 16
        G = 8
        EPS = 1e-05

        def _forward(x, prototypes, pos_embed, q_w, q_b, k_w, k_b, v_w, v_b, out_w, out_b, dw_w, bn_g, bn_b, bn_mean, bn_var, gn_g, gn_b):
            b, c, h, w = x.shape
            residual = x
            pos = jax.image.resize(pos_embed, (1, c, h, w), method='bilinear')
            xp = x + pos
            q = jnp.einsum('bchw,dc->bhwd', xp, q_w) + q_b
            q = q.reshape(b, h * w, c)
            k = prototypes[0] @ k_w.T + k_b
            v = prototypes[0] @ v_w.T + v_b
            scale = c ** (-0.5)
            attn = jax.nn.softmax(jnp.einsum('bnc,pc->bnp', q, k) * scale, axis=-1)
            out = jnp.einsum('bnp,pc->bnc', attn, v)
            out = out.reshape(b, h, w, c).transpose(0, 3, 1, 2)
            out = jnp.einsum('bchw,dc->bdhw', out, out_w) + out_b[None, :, None, None]
            dw = jax.lax.conv_general_dilated(out, dw_w, window_strides=(1, 1), padding='SAME', feature_group_count=c, dimension_numbers=('NCHW', 'OIHW', 'NCHW'))
            inv = (bn_g / jnp.sqrt(bn_var + EPS))[None, :, None, None]
            bn = (dw - bn_mean[None, :, None, None]) * inv + bn_b[None, :, None, None]
            out = out + jax.nn.gelu(bn, approximate=False)
            y = out + residual
            yg = y.reshape(b, G, c // G, h, w)
            mu = yg.mean(axis=(2, 3, 4), keepdims=True)
            var = yg.var(axis=(2, 3, 4), keepdims=True)
            yn = ((yg - mu) * jax.lax.rsqrt(var + EPS)).reshape(b, c, h, w)
            return yn * gn_g[None, :, None, None] + gn_b[None, :, None, None]
        return _forward(x, prototypes, pos_embed, q_w, q_b, k_w, k_b, v_w, v_b, out_w, out_b, dw_w, bn_g, bn_b, bn_mean, bn_var, gn_g, gn_b)

    def _gn(v, G=32, eps=1e-5):
        B_, C_, H_, W_ = v.shape
        g = v.reshape(B_, G, C_ // G, H_, W_)
        m = jnp.mean(g, axis=(2, 3, 4), keepdims=True)
        s = jnp.var(g, axis=(2, 3, 4), keepdims=True)
        return ((g - m) / jnp.sqrt(s + eps)).reshape(v.shape)

    def _ln_c(v, eps=1e-6):
        m = jnp.mean(v, axis=1, keepdims=True)
        s = jnp.var(v, axis=1, keepdims=True)
        return (v - m) / jnp.sqrt(s + eps)

    def _ln_t(v, eps=1e-5):
        m = jnp.mean(v, axis=-1, keepdims=True)
        s = jnp.var(v, axis=-1, keepdims=True)
        return (v - m) / jnp.sqrt(s + eps)

    def _to_tokens(v):
        B_, C_, H_, W_ = v.shape
        return v.reshape(B_, C_, H_ * W_).transpose(0, 2, 1)
    def _from_tokens(t, like):
        B_, C_, H_, W_ = like.shape
        return t.transpose(0, 2, 1).reshape(B_, C_, H_, W_)

    x = _L0_conv_ref(x, L0_conv_prototypes, L0_conv_pos_embed, L0_conv_q_w, L0_conv_q_b, L0_conv_k_w, L0_conv_k_b, L0_conv_v_w, L0_conv_v_b, L0_conv_out_w, L0_conv_out_b, L0_conv_dw_w, L0_conv_bn_g, L0_conv_bn_b, L0_conv_bn_mean, L0_conv_bn_var, L0_conv_gn_g, L0_conv_gn_b)
    return x


_drawn_inputs = setup_inputs


def setup_inputs(seed=0):
    import zlib

    import numpy as np

    out = dict(_drawn_inputs(seed))
    spreads = {}
    factors = {'L0_conv_pos_embed': 8.0,
     'L0_conv_q_b': 8.0,
     'L0_conv_k_b': 8.0,
     'L0_conv_v_b': 6.05,
     'L0_conv_out_b': 5.495,
     'L0_conv_bn_g': 2.709}
    for name, (base, spread) in spreads.items():
        noise = np.random.default_rng([zlib.crc32(name.encode()), seed]).standard_normal(out[name].shape)
        drawn = base * np.exp(spread * noise) if base else spread * noise
        out[name] = jnp.asarray(drawn.astype(out[name].dtype))
    for name, factor in factors.items():
        out[name] = (out[name] * factor).astype(out[name].dtype)
    return out
```

```python
from contextlib import ExitStack

import numpy as np

import concourse.bass as bass
from concourse import mybir

F32 = mybir.dt.float32
F16 = mybir.dt.float16
BF16 = mybir.dt.bfloat16
I32 = mybir.dt.int32
ALU = mybir.AluOpType
ACT = mybir.ActivationFunctionType
AX = mybir.AxisListType.X

B, C, H, W = 16, 256, 96, 96
NP = 16
POS = 64
P = 128
HALVES = C // P
GROUP = C // 8
EPS = 1e-5
ROWS = 32
COLS = 32
BLOCKS = H // ROWS
STRIPS = W // COLS
TILES = HALVES * STRIPS
PIX = ROWS * W
RING = 2 * BLOCKS
PAIRS = B // 2
LAST = B * BLOCKS
UNITS = BLOCKS * HALVES
JT = 4
JROWS = ROWS // JT
SLOT = 2 * NP
TW = W + 4
T2G = 4
PROB_SCALE = 1024.0
WT_SCALE = 256.0
UNSCALE = 1.0 / (PROB_SCALE * WT_SCALE)
PASSES = 2 * 3 + 1

Q_B, K_B, V_B, OUT_B, BN_G, BN_B, BN_MEAN, BN_VAR, GN_G, GN_B = range(10)


def build(nc, x, params, dw, qw, kwT, vwT, owT, protoT, pos, ident, group_mean, out):
    ctx = ExitStack()
    with ctx:
        def sb(name, shape, dt=F32):
            return ctx.enter_context(nc.sbuf_tensor(name, shape, dt))

        def sem(name):
            return ctx.enter_context(nc.semaphore(name))

        ring = sb("ring", [P, RING * HALVES * PIX])
        T = sb("T", [P, 2, ROWS, TW], F16)
        Z = sb("Z", [W, (H + 2) * 2 * SLOT], F16)
        L0 = sb("L0", [P, BLOCKS, JROWS * W])
        Ls = sb("Ls", [P, JROWS * W])
        E = sb("E", [W, ROWS, NP])
        A = sb("A", [W, ROWS, NP])
        G = sb("G", [P, 2, ROWS * COLS])
        junk = sb("junk", [P, PIX], BF16)
        Wt = sb("Wt", [P, HALVES * PASSES, P], F16)
        A32 = sb("A32", [P, HALVES, JT * 32])
        K32 = sb("K32", [P, HALVES, JT * 32])
        idf = sb("idf", [P, P])
        idh = sb("idh", [P, P], F16)
        gmat = sb("gmat", [P, P])
        par = sb("par", [P, 10, HALVES])
        dws = sb("dws", [P, HALVES, 9])
        pT = sb("pT", [P, HALVES, NP])
        vT = sb("vT", [P, HALVES, NP])
        mx = sb("mx", [W, ROWS])
        rs = sb("rs", [W, 2, ROWS])
        ysum = sb("ysum", [P, HALVES, BLOCKS * STRIPS])
        ysq = sb("ysq", [P, HALVES, BLOCKS * 2])
        tot = sb("tot", [P, 2, HALVES])
        gst = sb("gst", [P, 2, HALVES])
        aff = sb("aff", [P, 5, HALVES])
        neghalf = sb("neghalf", [P, HALVES])
        gs = sb("gs", [P, HALVES])
        gb = sb("gb", [P, HALVES])
        osc = sb("osc", [P, HALVES])
        bnw = sb("bnw", [P, 3, HALVES])
        mag = sb("mag", [P, 4, HALVES])
        l0c = sb("l0c", [P, 1])

        SL = HALVES * PIX
        P1 = ring[:, 2 * SL:2 * SL + POS * W].rearrange("p (y x) -> p y x", x=W)
        P0 = ring[:, 3 * SL:3 * SL + POS * POS].rearrange("p (y x) -> p y x", x=POS)
        s6y = ring[:, 3 * SL:3 * SL + POS * W].rearrange("p (y x) -> p y x", x=W)
        posS = ring[:, 4 * SL:4 * SL + HALVES * POS * POS].rearrange("p (h n) -> p h n", h=HALVES)
        s6x = ring[:, 4 * SL:4 * SL + POS * POS].rearrange("p (y x) -> p y x", x=POS)
        s2x = ring[:, 4 * SL + POS * POS:4 * SL + POS * POS * 3 // 2].rearrange("p (y x) -> p y x", x=POS // 2)
        P2 = ring[:, 4 * SL:4 * SL + H * W].rearrange("p (y x) -> p y x", x=W)
        tail = ring[:, 4 * SL + H * W:6 * SL]
        s2y = tail[:, 0:POS // 2 * W].rearrange("p (y x) -> p y x", x=W)
        wS = [tail[:, n * HALVES * C:(n + 1) * HALVES * C].rearrange("p (h n) -> p h n", h=HALVES) for n in range(4)]
        qwS, kwS, vwS, owS = wS
        Wf = G[:, 0, 0:HALVES * PASSES * P // 2].bitcast(F16).rearrange(
            "p (h q s c n) -> p h q s c n", h=HALVES, q=PASSES, s=4, c=2)
        CW = G[:, 1, 0:HALVES * 10 * NP].rearrange("p (h t n) -> p h t n", h=HALVES, n=NP)
        Whi = G[:, 1, 320:480].bitcast(F16).rearrange("p (h t n) -> p h t n", h=HALVES, n=NP)
        Wlo = G[:, 1, 480:640].bitcast(F16).rearrange("p (h t n) -> p h t n", h=HALVES, n=NP)

        conv_ps = ctx.enter_context(nc.psum_tensor("conv_ps", [P, 2, 2, 512], F32))
        out_ps = ctx.enter_context(nc.psum_tensor("out_ps", [P, 2, 512], F32))
        lg_ps = ctx.enter_context(nc.psum_tensor("lg_ps", [P, 512], F32))
        tr_ps = ctx.enter_context(nc.psum_tensor("tr_ps", [P, 512], F32))
        tr16 = tr_ps[:, :].bitcast(F16)

        small_in, weights_in, pos_in = sem("small_in"), sem("weights_in"), sem("pos_in")
        x_in = [sem(f"x_in{k}") for k in range(RING)]
        stored = [sem(f"stored{k}") for k in range(RING * HALVES)]
        pe_setup, vec_setup, act_setup, pool_setup = sem("pe_setup"), sem("vec_setup"), sem("act_setup"), sem("pool_setup")
        vec_step, pool_step = sem("vec_step"), sem("pool_step")
        conv_done, out_done = sem("conv_done"), sem("out_done")
        gelu_done = sem("gelu_done")
        out_added, y_done = sem("out_added"), sem("y_done")
        lg_done, lg_copied = sem("lg_done"), sem("lg_copied")
        t1_done, max_done, sub_done = sem("t1_done"), sem("max_done"), sem("sub_done")
        exp_done, soft_step, probs_ready = sem("exp_done"), sem("soft_step"), sem("probs_ready")
        t2_done, t2_copied = sem("t2_done"), sem("t2_copied")
        sq_done = sem("sq_done")
        tot_done, group_done, group_copied = sem("tot_done"), sem("group_done"), sem("group_copied")
        norm_done = sem("norm_done")

        PE_KV, PE_A, PE_POS, PE_WT = 1, 2, 3, 3 + POS * POS // 512
        VEC_KV, VEC_A, VEC_WF, VEC_WT, VEC_P1, VEC_P2, VEC_L0 = range(1, 8)

        def until(eng, semaphore, value):
            if not isinstance(value, int) or value > 0:
                eng.wait_ge(semaphore, value)

        def halves(k):
            return ring[:, k * SL:(k + 1) * SL].rearrange("p (h y x) -> p h y x", h=HALVES, x=W)

        def passes(eng, body):
            body(0)
            with eng.Fori(1, PAIRS - 1) as i:
                body(i)
            body(PAIRS - 1)

        def fronted(t):
            return not isinstance(t, int) or t < LAST

        block = ctx.enter_context(nc.Block())

        @block.sync
        def _(sp):
            def unit(dram, b, u):
                return dram[b, (u % HALVES) * P:(u % HALVES + 1) * P, (u // HALVES) * ROWS:(u // HALVES + 1) * ROWS, :]\
                    .rearrange("c y x -> c (y x)")

            def place(j, u):
                at = (j * UNITS + u) * PIX
                return ring[:, at:at + PIX]

            def load(b, j, u):
                sp.dma_start(place(j, u), unit(x, b, u)).then_inc(x_in[j * BLOCKS + u // HALVES], 16)

            sp.dma_start(par[:, :, :], params).then_inc(small_in, 16)
            sp.dma_start(pT[:, :, :], protoT.rearrange("(h p) n -> p h n", p=P)).then_inc(small_in, 16)
            for dst, src in ((kwS, kwT), (vwS, vwT), (qwS, qw), (owS, owT)):
                sp.dma_start(dst, src.rearrange("(h p) n -> p h n", p=P)).then_inc(weights_in, 16)
            sp.dma_start(dws[:, :, :], dw).then_inc(small_in, 16)
            sp.dma_start(idf[:, :], ident).then_inc(small_in, 16)
            sp.dma_start(gmat[:, :], group_mean).then_inc(small_in, 16)
            sp.dma_start(posS, pos.rearrange("(h p) n -> p h n", p=P)).then_inc(pos_in, 16)
            for u in range(2 * HALVES):
                load(0, 0, u)
            sp.wait_ge(vec_setup, VEC_P2)
            for u in range(2 * HALVES, UNITS + HALVES):
                load(u // UNITS, u // UNITS, u % UNITS)
            sp.wait_ge(vec_setup, VEC_L0)
            for u in range(HALVES, UNITS):
                load(1, 1, u)

            def store_and_reload(i, j, count, reload):
                for u in range(UNITS + 1):
                    if u < UNITS:
                        until(sp, norm_done, UNITS * (2 * i + j) + u + 1)
                        sp.dma_start(unit(out, 2 * i + j, u), place(j, u)).then_inc(stored[j * UNITS + u], 16)
                    if u and reload:
                        until(sp, stored[j * UNITS + u - 1], 16 * (i + 1))
                        load(2 * i + j + 2, j, u - 1)

            store_and_reload(0, 0, 0, True)
            with sp.Fori(1, PAIRS - 1) as i:
                store_and_reload(i - 1, 1, 0, True)
                store_and_reload(i, 0, 0, True)
            store_and_reload(PAIRS - 2, 1, 0, True)
            store_and_reload(PAIRS - 1, 0, 0, False)
            store_and_reload(PAIRS - 1, 1, 0, False)
            for u in range(RING * HALVES):
                sp.wait_ge(stored[u], 16 * PAIRS)

        @block.gpsimd
        def _(pool):
            nc.gpsimd.memset(K32[:, :, :], 0.0)
            nc.gpsimd.memset(A32[:, :, :], 0.0)
            nc.gpsimd.memset(Wf, 0.0)
            nc.gpsimd.memset(ysq[:, :, :], 0.0)
            nc.gpsimd.memset(neghalf[:, :], -0.5).then_inc(pool_setup, 1)
            nc.gpsimd.memset(Z[:, 0:2 * SLOT], 0.0)
            nc.gpsimd.memset(Z[:, (H + 1) * 2 * SLOT:(H + 2) * 2 * SLOT], 0.0)
            for k in range(2):
                nc.gpsimd.memset(T[:, k, :, 0:2], 0.0)
                nc.gpsimd.memset(T[:, k, :, TW - 2:TW], 0.0)
            pool.wait_ge(small_in, 80)
            nc.gpsimd.tensor_scalar(bnw[:, 0, :], par[:, BN_VAR, :], EPS, None, ALU.add).then_inc(pool_step, 1)
            pool.wait_ge(pool_step, 1)
            pool.wait_ge(pool_setup, 1)
            nc.gpsimd.tensor_tensor(bnw[:, 1, :], bnw[:, 0, :], neghalf[:, :], ALU.pow).then_inc(pool_step, 1)
            pool.wait_ge(pool_step, 2)
            nc.gpsimd.tensor_tensor(bnw[:, 2, :], bnw[:, 1, :], par[:, BN_G, :], ALU.mult).then_inc(pool_setup, 1)

            def normalise(b, j):
                until(pool, group_copied, b + 1)
                mean, msq = gst[:, 0, :], gst[:, 1, :]

                def step(n, inst):
                    pool.drain()

                step(0, nc.gpsimd.tensor_tensor(aff[:, 0, :], mean, mean, ALU.mult))
                step(1, nc.gpsimd.tensor_tensor(aff[:, 0, :], msq, aff[:, 0, :], ALU.subtract))
                step(2, nc.gpsimd.tensor_scalar(aff[:, 0, :], aff[:, 0, :], 0.0, EPS, ALU.max, ALU.add))
                step(3, nc.gpsimd.tensor_tensor(aff[:, 1, :], aff[:, 0, :], neghalf[:, :], ALU.pow))
                step(4, nc.gpsimd.tensor_tensor(aff[:, 2, :], aff[:, 1, :], par[:, GN_G, :], ALU.mult))
                step(5, nc.gpsimd.tensor_tensor(aff[:, 3, :], aff[:, 2, :], mean, ALU.mult))
                step(6, nc.gpsimd.tensor_tensor(aff[:, 4, :], par[:, GN_B, :], aff[:, 3, :], ALU.subtract))
                for u in range(UNITS):
                    h = u % HALVES
                    at_u = ring[:, (j * UNITS + u) * PIX:(j * UNITS + u + 1) * PIX]
                    nc.gpsimd.tensor_scalar(at_u, at_u, aff[:, 2, h:h + 1], aff[:, 4, h:h + 1],
                                            ALU.mult, ALU.add).then_inc(norm_done, 1)

            normalise(0, 0)
            with pool.Fori(1, PAIRS - 1) as i:
                normalise(2 * i - 1, 1)
                normalise(2 * i, 0)
            for b in (B - 3, B - 2, B - 1):
                normalise(b, b % 2)

        @block.tensor
        def _(pe):
            small = conv_ps[:, 0, 0, :]
            pe.wait_ge(small_in, 80)
            pe.wait_ge(weights_in, 64)
            for n, w in enumerate((kwS, vwS)):
                for dh in range(HALVES):
                    for ch in range(HALVES):
                        last = nc.tensor.matmul(small[:, (2 * n + dh) * NP:(2 * n + dh + 1) * NP],
                                                w[:, ch, dh * P:(dh + 1) * P], pT[:, ch, :],
                                                start=ch == 0, stop=ch == HALVES - 1)
            last.then_inc(pe_setup, 1)
            pe.wait_ge(vec_setup, VEC_KV)
            second = conv_ps[:, 0, 1, :]
            for n, (w, r) in enumerate(((qwS, K32), (owS, vT))):
                for ch in range(HALVES):
                    for dh in range(HALVES):
                        nc.tensor.matmul(second[:, (2 * n + ch) * NP:(2 * n + ch + 1) * NP],
                                         w[:, dh, ch * P:(ch + 1) * P], r[:, dh, 0:NP],
                                         start=dh == 0, stop=dh == HALVES - 1)
            for dh in range(HALVES):
                last = nc.tensor.matmul(second[:, 64:65], K32[:, dh, :], par[:, Q_B, dh:dh + 1],
                                        start=dh == 0, stop=dh == HALVES - 1)
            last.then_inc(pe_setup, 1)
            pe.wait_ge(vec_setup, VEC_A)
            pe.wait_ge(pos_in, 16)
            pos_banks = [out_ps[:, 0, :], out_ps[:, 1, :], conv_ps[:, 1, 0, :], conv_ps[:, 1, 1, :]]
            for n in range(POS * POS // 512):
                if n >= 4:
                    pe.wait_ge(act_setup, n - 3)
                for ch in range(HALVES):
                    last = nc.tensor.matmul(pos_banks[n % 4], A32[:, ch, :], posS[:, ch, n * 512:(n + 1) * 512],
                                            start=ch == 0, stop=ch == HALVES - 1)
                last.then_inc(pe_setup, 1)
            pe.wait_ge(vec_setup, VEC_WF)
            for h in range(HALVES):
                turned = conv_ps[:, 0, h, :].bitcast(F16)
                for q in range(PASSES):
                    last = nc.tensor.transpose(turned[:, q * P:(q + 1) * P],
                                               Wf[:, h, q].rearrange("p s c n -> p (s c n)"), idh[:, :])
            last.then_inc(pe_setup, 1)

            def logits(m, k, g):
                if g == 0:
                    pair = (m - k) // RING if isinstance(m, int) else None
                until(pe, x_in[k], x_count(m, k))
                until(pe, sub_done, 2 * m + g)
                xs = halves(k)
                for ch in range(HALVES):
                    for j in range(JT):
                        r0 = j * JROWS + g * (JROWS // 2)
                        last = nc.tensor.matmul(lg_ps[32 * j:32 * j + 32, 0:JROWS // 2 * W], A32[:, ch, 0:32],
                                                xs[:, ch, r0:r0 + JROWS // 2, :],
                                                start=ch == 0, stop=ch == HALVES - 1)
                last.then_inc(lg_done, 1)

            def x_count(m, k):
                return x_of(m, k)

            def x_of(m, k):
                return 32 * ((m - k) // RING + 1) if isinstance(m, int) else m_pair[0] * 32 + 32

            m_pair = [None]

            def turn_logits(m, g):
                until(pe, lg_copied, 2 * m + g + 1)
                for i in range(JROWS // 2):
                    r = g * (JROWS // 2) + i
                    last = nc.tensor.transpose(lg_ps[0:W, i * P:(i + 1) * P], Ls[:, r * W:(r + 1) * W], idf[:, :])
                last.then_inc(t1_done, 1)

            def turn_probs(t, kb, g):
                if g == T2G - 1 and kb < BLOCKS - 1:
                    until(pe, probs_ready, t + 2)
                elif g == 0:
                    until(pe, probs_ready, t + 1)
                until(pe, t2_copied, T2G * t + g)
                for r in range(ROWS // T2G):
                    y = kb * ROWS + g * (ROWS // T2G) + r
                    last = nc.tensor.transpose(tr16[:, r * W:(r + 1) * W],
                                               Z[:, (2 * y + 1) * SLOT:(2 * y + 1) * SLOT + 4 * SLOT], idh[0:W, 0:W])
                last.then_inc(t2_done, 1)

            def group_means(b):
                until(pe, tot_done, 2 * (b + 1))
                nc.tensor.matmul(tr_ps[:, 0:2 * HALVES], gmat[:, :], tot[:, :, :].rearrange("p a h -> p (a h)"),
                                 start=True, stop=True).then_inc(group_done, 1)

            def conv_half(n, h, s, buf, row_half):
                for dx in range(3):
                    for part in range(2):
                        last = nc.tensor.matmul(
                            conv_ps[:, n % 2, row_half, :], Wt[:, h * PASSES + 2 * dx + part, :],
                            T[:, buf, row_half * 16:row_half * 16 + 16, 1 + s * COLS + dx:1 + s * COLS + dx + COLS],
                            start=dx == 0 and part == 0, stop=dx == 2 and part == 1)
                return last

            pe.wait_ge(vec_setup, VEC_L0)
            pe.wait_ge(vec_setup, VEC_WT)
            for m in range(2):
                for g in range(2):
                    logits(m, m, g)
                    turn_logits(m, g)
            pe.wait_ge(pool_setup, 2)
            for g in range(T2G):
                turn_probs(0, 0, g)

            def body(i):
                for k in range(RING):
                    t, kb, m, mk = RING * i + k, k % BLOCKS, RING * i + k + 2, (k + 2) % RING
                    m_pair[0] = i + (k + 2) // RING
                    for n in range(TILES):
                        h, s = divmod(n, STRIPS)
                        at = TILES * t + n
                        if n == 0:
                            until(pe, t2_copied, T2G * (t + 1))
                        until(pe, gelu_done, at - 1)
                        conv_half(n, h, s, k % 2, 0)
                        if n == 0 and fronted(m):
                            logits(m, mk, 0)
                        if n == 1 and fronted(m):
                            turn_logits(m, 0)
                        if n == 1 and kb == 0 and not (isinstance(t, int) and t == 0):
                            until(pe, t2_copied, T2G * (t + 1) + 1)
                            group_means(2 * i + k // BLOCKS - 1)
                        conv_half(n, h, s, k % 2, 1).then_inc(conv_done, 1)
                        until(pe, out_added, at)
                        for row_half in range(2):
                            last = nc.tensor.matmul(
                                out_ps[:, row_half, :], Wt[:, h * PASSES + PASSES - 1, :],
                                T[:, k % 2, row_half * 16:row_half * 16 + 16, 2 + s * COLS:2 + s * COLS + COLS],
                                start=True, stop=True)
                        last.then_inc(out_done, 1)
                        if n == 1 and fronted(m):
                            logits(m, mk, 1)
                        if n == 2 and fronted(m):
                            turn_logits(m, 1)
                        if fronted(t + 1):
                            if n < 3:
                                if n == 1 and kb == 0 and not (isinstance(t, int) and t == 0):
                                    until(pe, group_copied, 2 * i + k // BLOCKS)
                                turn_probs(t + 1, (k + 1) % BLOCKS, n)
                            if n == 4:
                                turn_probs(t + 1, (k + 1) % BLOCKS, 3)

            passes(pe, body)
            group_means(B - 1)

        @block.scalar
        def _(act):
            pos_banks = [out_ps[:, 0, :], out_ps[:, 1, :], conv_ps[:, 1, 0, :], conv_ps[:, 1, 1, :]]
            for n in range(POS * POS // 512):
                act.wait_ge(pe_setup, PE_POS + n)
                nc.scalar.activation(P0[:, n * 8:(n + 1) * 8, :].rearrange("p y x -> p (y x)"), pos_banks[n % 4],
                                     ACT.Copy).then_inc(act_setup, 1)
            act.wait_ge(vec_setup, VEC_L0)
            act.wait_ge(pool_setup, 2)

            def exponent(m):
                act.wait_ge(sub_done, 2 * m + 2)
                nc.scalar.activation(E[:, :, :], E[:, :, :], ACT.Exp).then_inc(exp_done, 1)

            def copy_probs(t, buf, g):
                if g == 0:
                    until(act, out_done, TILES * (t - 1))
                act.wait_ge(t2_done, T2G * t + g + 1)
                nc.scalar.activation(T[:, buf, g * 8:(g + 1) * 8, 2:2 + W],
                                     tr16[:, 0:8 * W].rearrange("p (y x) -> p y x", x=W), ACT.Copy)\
                    .then_inc(t2_copied, 1)

            def square(k, h, c0, c1, slot, count, before):
                act.wait_ge(y_done, count)
                until(act, sq_done, before)
                src = halves(k)[:, h, :, c0:c1]
                nc.scalar.activation(junk[:, 0:ROWS * (c1 - c0)].rearrange("p (y x) -> p y x", y=ROWS), src, ACT.Square,
                                     accum_out=ysq[:, h, (k % BLOCKS) * 2 + slot:(k % BLOCKS) * 2 + slot + 1])\
                    .then_inc(sq_done, 1)

            exponent(0)
            exponent(1)
            for g in range(T2G):
                copy_probs(0, 0, g)

            def body(i):
                for k in range(RING):
                    t = RING * i + k
                    for n in range(TILES):
                        h, s = divmod(n, STRIPS)
                        at = TILES * t + n
                        if n == 0 and not (isinstance(t, int) and t == 0):
                            square((k - 1) % RING, 1, 2 * COLS, W, 1, TILES * t, 3 * t - 1)
                        if n == 3 and fronted(t + 2):
                            exponent(t + 2)
                        act.wait_ge(conv_done, at + 1)
                        until(act, y_done, at - 1)
                        nc.scalar.activation(G[:, n % 2, :], conv_ps[:, n % 2, :, :].rearrange("p a b -> p (a b)"),
                                             ACT.Gelu, bias=gb[:, h:h + 1], scale=gs[:, h:h + 1])\
                            .then_inc(gelu_done, 1)
                        if fronted(t + 1):
                            if n < 3:
                                copy_probs(t + 1, (k + 1) % 2, n)
                            if n == 5:
                                copy_probs(t + 1, (k + 1) % 2, 3)
                        if n == 4:
                            square(k, 0, 0, W, 0, TILES * t + 3, 3 * t)
                        if n == 5:
                            square(k, 1, 0, 2 * COLS, 0, TILES * t + 5, 3 * t + 1)

            passes(act, body)
            square(RING - 1, 1, 2 * COLS, W, 1, TILES * LAST, 3 * LAST - 1)

        @block.vector
        def _(dve):
            count = [0]

            def step(inst):
                count[0] += 1
                inst.then_inc(vec_step, 1)
                dve.wait_ge(vec_step, count[0])

            small = conv_ps[:, 0, 0, :]
            second = conv_ps[:, 0, 1, :]
            dve.wait_ge(small_in, 80)
            dve.wait_ge(pool_setup, 1)
            nc.vector.tensor_copy(idh[:, :], idf[:, :])
            dve.wait_ge(pe_setup, PE_KV)
            for dh in range(HALVES):
                nc.vector.tensor_scalar(K32[:, dh, :].rearrange("p (j n) -> p j n", n=32)[:, :, 0:NP],
                                        small[:, dh * NP:(dh + 1) * NP].unsqueeze(1).to_broadcast([P, JT, NP]),
                                        par[:, K_B, dh:dh + 1], C ** -0.5, ALU.add, ALU.mult)
                last = nc.vector.tensor_scalar(vT[:, dh, :], small[:, (2 + dh) * NP:(3 + dh) * NP],
                                               par[:, V_B, dh:dh + 1], None, ALU.add)
            last.then_inc(vec_setup, 1)
            dve.wait_ge(pe_setup, PE_A)
            for ch in range(HALVES):
                last = nc.vector.tensor_copy(A32[:, ch, :].rearrange("p (j n) -> p j n", n=32)[:, :, 0:NP],
                                             second[:, ch * NP:(ch + 1) * NP].unsqueeze(1).to_broadcast([P, JT, NP]))
            last.then_inc(vec_setup, 1)
            nc.vector.tensor_copy(l0c[:, :], second[:, 64:65])

            for h in range(HALVES):
                last = nc.vector.tensor_scalar(CW[:, h, 9, :], second[:, (2 + h) * NP:(3 + h) * NP],
                                               par[:, OUT_B, h:h + 1], None, ALU.add)
            step(last)
            for h in range(HALVES):
                last = nc.vector.tensor_tensor(CW[:, h, 0:9, :], CW[:, h, 9:10, :].to_broadcast([P, 9, NP]),
                                               dws[:, h, :].unsqueeze(2).to_broadcast([P, 9, NP]), ALU.mult)
            step(last)
            nc.vector.tensor_reduce(mag[:, 0, :], CW[:, :, 0:9, :].rearrange("p h t n -> p h (t n)"), AX, ALU.max,
                                    apply_absolute_value=True)
            step(nc.vector.tensor_reduce(mag[:, 1, :], CW[:, :, 9, :], AX, ALU.max, apply_absolute_value=True))
            step(nc.vector.tensor_scalar(mag[:, 0:2, :], mag[:, 0:2, :], 1e-30, None, ALU.max))
            step(nc.vector.tensor_scalar(mag[:, 0:2, :].bitcast(I32), mag[:, 0:2, :].bitcast(I32), 0x7F800000, None,
                                         ALU.bitwise_and))
            step(nc.vector.reciprocal(mag[:, 2:4, :], mag[:, 0:2, :]))
            for h in range(HALVES):
                nc.vector.tensor_scalar(CW[:, h, 0:9, :], CW[:, h, 0:9, :], mag[:, 2, h:h + 1], WT_SCALE,
                                        ALU.mult, ALU.mult)
                last = nc.vector.tensor_scalar(CW[:, h, 9, :], CW[:, h, 9, :], mag[:, 3, h:h + 1], WT_SCALE,
                                               ALU.mult, ALU.mult)
            step(last)
            step(nc.vector.tensor_copy(Whi, CW))
            step(nc.vector.tensor_tensor(Wlo, CW, Whi, ALU.subtract))
            for h in range(HALVES):
                def fill(q, slot, src, tap):
                    return nc.vector.tensor_copy(Wf[:, h, q, slot], src[:, h, tap:tap + 1, :].to_broadcast([P, 2, NP]))
                for dx in range(3):
                    fill(2 * dx, 0, Whi, dx)
                    fill(2 * dx, 1, Whi, 3 + dx)
                    fill(2 * dx, 2, Wlo, 3 + dx)
                    fill(2 * dx, 3, Whi, 6 + dx)
                    fill(2 * dx + 1, 0, Wlo, dx)
                    fill(2 * dx + 1, 3, Wlo, 6 + dx)
                fill(PASSES - 1, 1, Whi, 9)
                last = fill(PASSES - 1, 2, Wlo, 9)
            last.then_inc(vec_setup, 1)
            dve.wait_ge(pool_setup, 2)
            step(nc.vector.tensor_tensor(gb[:, :], par[:, BN_MEAN, :], bnw[:, 2, :], ALU.mult))
            nc.vector.tensor_tensor(gb[:, :], par[:, BN_B, :], gb[:, :], ALU.subtract)
            step(nc.vector.tensor_tensor(gs[:, :], mag[:, 0, :], bnw[:, 2, :], ALU.mult))
            nc.vector.tensor_scalar(gs[:, :], gs[:, :], UNSCALE, None, ALU.mult)
            nc.vector.tensor_scalar(osc[:, :], mag[:, 1, :], UNSCALE, None, ALU.mult)
            dve.wait_ge(pe_setup, PE_WT)
            for h in range(HALVES):
                last = nc.vector.tensor_copy(Wt[:, h * PASSES:(h + 1) * PASSES, :].rearrange("p q c -> p (q c)"),
                                             conv_ps[:, 0, h, :].bitcast(F16)[:, 0:PASSES * P])
            last.then_inc(vec_setup, 1)

            def resize(dst, src, sixth, half, at):
                m = POS // 2

                def mix(o, whole, part, by):
                    return nc.vector.scalar_tensor_tensor(out=o, in0=whole, scalar=by, in1=part, op0=ALU.mult, op1=ALU.add)
                nc.vector.tensor_scalar(sixth, src, 1.0 / 6.0, None, ALU.mult)
                nc.vector.tensor_copy(at(dst, 0, 1), at(src, 0, 1))
                nc.vector.tensor_copy(at(dst, 3 * m - 1, 3 * m), at(src, 2 * m - 1, 2 * m))
                step(nc.vector.tensor_scalar(half, at(src, 1, 2 * m, 2), 0.5, None, ALU.mult))
                mix(at(dst, 3, 3 * m, 3), at(src, 2, 2 * m, 2), at(sixth, 1, 2 * m - 1, 2), 5.0 / 6.0)
                mix(at(dst, 1, 3 * m, 3), at(src, 0, 2 * m, 2), half, 0.5)
                return mix(at(dst, 2, 3 * m - 1, 3), at(src, 1, 2 * m - 1, 2), at(sixth, 2, 2 * m, 2), 5.0 / 6.0)

            def cols(a, lo, hi, by=1):
                return a[:, :, lo:hi:by]

            def rows(a, lo, hi, by=1):
                return a[:, lo:hi:by, :]

            dve.wait_ge(act_setup, POS * POS // 512)
            resize(P1, P0, s6x, s2x, cols).then_inc(vec_setup, 1)
            dve.wait_ge(vec_setup, VEC_P1)
            resize(P2, P1, s6y, s2y, rows).then_inc(vec_setup, 1)
            dve.wait_ge(vec_setup, VEC_P2)
            for kb in range(BLOCKS):
                for j in range(JT):
                    r0 = kb * ROWS + j * JROWS
                    last = nc.vector.tensor_scalar(L0[32 * j:32 * j + 32, kb, :],
                                                   P2[32 * j:32 * j + 32, r0:r0 + JROWS, :].rearrange("p y x -> p (y x)"),
                                                   l0c[32 * j:32 * j + 32, :], None, ALU.add)
            last.then_inc(vec_setup, 1)
            dve.wait_ge(vec_setup, VEC_L0)

            HALF = JROWS // 2 * W

            def add_l0(m, kb, g):
                dve.wait_ge(lg_done, 2 * m + g + 1)
                until(dve, t1_done, 2 * m + g - 1)
                nc.vector.tensor_tensor(Ls[:, g * HALF:(g + 1) * HALF], lg_ps[:, 0:HALF],
                                        L0[:, kb, g * HALF:(g + 1) * HALF], ALU.add).then_inc(lg_copied, 1)

            def subtract_max(m, g):
                dve.wait_ge(t1_done, 2 * m + g + 1)
                lg = lg_ps[0:W, :].rearrange("x (i j n) -> x i j n", i=JROWS // 2, n=32)[:, :, :, 0:NP]
                most = mx[:, g * 16:(g + 1) * 16].rearrange("x (i j) -> x i j", j=JT)
                nc.vector.tensor_reduce(most, lg, AX, ALU.max).then_inc(max_done, 1)
                dve.wait_ge(max_done, 2 * m + g + 1)
                dst = E[:, :, :].rearrange("x (j i) n -> x i j n", i=JROWS)[:, g * 4:(g + 1) * 4]
                nc.vector.tensor_tensor(dst, lg, most.unsqueeze(3).to_broadcast([W, JROWS // 2, JT, NP]),
                                        ALU.subtract).then_inc(sub_done, 1)

            SOFT = 5

            def softmax(m, kb):
                at = SOFT * m

                def chain(n, inst):
                    inst.then_inc(soft_step, 1)
                    dve.wait_ge(soft_step, at + n + 1)
                dve.wait_ge(exp_done, m + 1)
                chain(0, nc.vector.tensor_reduce(rs[:, 0, :], E[:, :, :], AX, ALU.add))
                chain(1, nc.vector.reciprocal(rs[:, 1, :], rs[:, 0, :]))
                chain(2, nc.vector.scalar_tensor_tensor(out=A[:, :, :], in0=E[:, :, :], scalar=PROB_SCALE,
                                                        in1=rs[:, 1, :].unsqueeze(2).to_broadcast([W, ROWS, NP]),
                                                        op0=ALU.mult, op1=ALU.mult))
                r0 = 1 + kb * ROWS
                z = Z[:, r0 * 2 * SLOT:(r0 + ROWS) * 2 * SLOT].rearrange("x (y d c n) -> x y d c n", d=2, c=2, n=NP)
                until(dve, t2_done, T2G * (m - 2))
                chain(3, nc.vector.tensor_copy(z[:, :, 0, 0, :], A[:, :, :]))
                chain(4, nc.vector.tensor_tensor(z[:, :, 0, 1, :], A[:, :, :], z[:, :, 0, 0, :], ALU.subtract))
                zz = Z[:, r0 * 2 * SLOT:(r0 + ROWS) * 2 * SLOT].rearrange("x (y d n) -> x y d n", d=2, n=SLOT)
                nc.vector.tensor_copy(zz[:, :, 1, :], zz[:, :, 0, :]).then_inc(probs_ready, 1)

            def add_out(k, n, at):
                h, s = divmod(n, STRIPS)
                dve.wait_ge(out_done, at + 1)
                v = halves(k)[:, h, :, s * COLS:(s + 1) * COLS]
                nc.vector.scalar_tensor_tensor(out=v, in0=out_ps[:, :, :].rearrange("p a (y x) -> p (a y) x", x=COLS),
                                               scalar=osc[:, h:h + 1], in1=v, op0=ALU.mult, op1=ALU.add)\
                    .then_inc(out_added, 1)

            def add_gelu(k, n, at):
                h, s = divmod(n, STRIPS)
                dve.wait_ge(gelu_done, at + 1)
                dve.wait_ge(out_added, at + 1)
                v = halves(k)[:, h, :, s * COLS:(s + 1) * COLS]
                c = (k % BLOCKS) * STRIPS + s
                nc.vector.scalar_tensor_tensor(out=v, in0=G[:, n % 2, :].rearrange("p (y x) -> p y x", x=COLS), scalar=1.0,
                                               in1=v, op0=ALU.mult, op1=ALU.add, accum_out=ysum[:, h, c:c + 1])\
                    .then_inc(y_done, 1)

            def sum_image(t, b):
                dve.wait_ge(sq_done, 3 * t)
                dve.wait_ge(y_done, TILES * t)
                nc.vector.tensor_reduce(tot[:, 0, :], ysum[:, :, :], AX, ALU.add).then_inc(tot_done, 1)
                nc.vector.tensor_reduce(tot[:, 1, :], ysq[:, :, :], AX, ALU.add).then_inc(tot_done, 1)
                dve.wait_ge(tot_done, 2 * (b + 1))

            def take_means(b):
                dve.wait_ge(group_done, b + 1)
                until(dve, norm_done, UNITS * (b - 1) + 1)
                nc.vector.tensor_copy(gst[:, :, :].rearrange("p a h -> p (a h)"), tr_ps[:, 0:2 * HALVES])\
                    .then_inc(group_copied, 1)

            for m in range(2):
                for g in range(2):
                    add_l0(m, m, g)
                    subtract_max(m, g)
                softmax(m, m)

            def body(i):
                for k in range(RING):
                    t, m = RING * i + k, RING * i + k + 2
                    mb = (k + 2) % BLOCKS
                    b = 2 * i + k // BLOCKS - 1
                    image_ended = k % BLOCKS == 0 and not (isinstance(t, int) and t == 0)
                    for n in range(TILES):
                        at = TILES * t + n
                        if n == 1 and image_ended:
                            sum_image(t, b)
                        if not (n == 0 and isinstance(t, int) and t == 0):
                            add_gelu((k - (n == 0)) % RING, (n - 1) % TILES, at - 1)
                        if fronted(m):
                            if n == 0:
                                add_l0(m, mb, 0)
                            if n == 1:
                                subtract_max(m, 0)
                            if n == 2:
                                add_l0(m, mb, 1)
                            if n == 3:
                                subtract_max(m, 1)
                            if n == 4:
                                softmax(m, mb)
                        if n == 1 and image_ended:
                            take_means(b)
                        add_out(k, n, at)

            passes(dve, body)
            add_gelu(RING - 1, TILES - 1, TILES * LAST - 1)
            sum_image(LAST, B - 1)
            take_means(B - 1)


def kernel(**inputs):
    import concourse.bacc as bacc
    from concourse.bass_utils import run_bass_kernel_spmd

    a = {k.removeprefix("L0_conv_"): np.asarray(v) for k, v in inputs.items()}
    vectors = np.stack([a[n] for n in ("q_b", "k_b", "v_b", "out_b", "bn_g", "bn_b", "bn_mean", "bn_var", "gn_g", "gn_b")])
    same_group = np.kron(np.eye(P // GROUP), np.ones((GROUP, GROUP)))
    arrays = {
        "x": a["x"],
        "params": vectors.reshape(10, HALVES, P).transpose(2, 0, 1),
        "dw": a["dw_w"].reshape(HALVES, P, 9).transpose(1, 0, 2),
        "qw": a["q_w"],
        "kwT": a["k_w"].T,
        "vwT": a["v_w"].T,
        "owT": a["out_w"].T,
        "protoT": a["prototypes"][0].T,
        "pos": a["pos_embed"].reshape(C, POS * POS),
        "ident": np.eye(P, dtype=np.float32),
        "group_mean": (same_group / (GROUP * H * W)).astype(np.float32),
    }
    arrays = {f"in_{k}": np.ascontiguousarray(v) for k, v in arrays.items()}
    nc = bacc.Bacc("TRN2", target_bir_lowering=False, num_devices=1)
    args = [nc.dram_tensor(k, v.shape, mybir.dt.from_np(v.dtype), kind="ExternalInput").ap() for k, v in arrays.items()]
    out = nc.dram_tensor("out", (B, C, H, W), F32, kind="ExternalOutput").ap()
    build(nc, *args, out)
    r = run_bass_kernel_spmd(nc, [arrays], core_ids=[0])
    return r.results[0]["out"]
```

```python
from contextlib import ExitStack

import numpy as np

import concourse.bass as bass
from concourse import mybir

F32 = mybir.dt.float32
F16 = mybir.dt.float16
BF16 = mybir.dt.bfloat16
I32 = mybir.dt.int32
ALU = mybir.AluOpType
ACT = mybir.ActivationFunctionType
AX = mybir.AxisListType.X

B, C, H, W = 16, 256, 96, 96
NP = 16
POS = 64
P = 128
HALVES = C // P
GROUP = C // 8
EPS = 1e-5
ROWS = 32
COLS = 32
BLOCKS = H // ROWS
STRIPS = W // COLS
TILES = HALVES * STRIPS
PIX = ROWS * W
RING = 2 * BLOCKS
PAIRS = B // 2
LAST = B * BLOCKS
HROWS = ROWS // 2
SPANS = [(0, HROWS, 0), (0, HROWS, 1), (HROWS, HROWS, 0), (HROWS, HROWS, 1)]
SPANS += [(kb * ROWS, ROWS, h) for kb in range(1, BLOCKS) for h in range(HALVES)]
UNITS = len(SPANS)
JT = 4
JROWS = ROWS // JT
SLOT = 2 * NP
TW = W + 4
T2G = 4
PROB_SCALE = 1024.0
WT_SCALE = 256.0
UNSCALE = 1.0 / (PROB_SCALE * WT_SCALE)
PASSES = 2 * 3 + 1

Q_B, K_B, V_B, OUT_B, BN_G, BN_B, BN_MEAN, BN_VAR, GN_G, GN_B = range(10)


def build(nc, x, params, dw, qw, kwT, vwT, owT, protoT, pos, ident, group_mean, out):
    ctx = ExitStack()
    with ctx:
        def sb(name, shape, dt=F32):
            return ctx.enter_context(nc.sbuf_tensor(name, shape, dt))

        def sem(name):
            return ctx.enter_context(nc.semaphore(name))

        ring = sb("ring", [P, RING * HALVES * PIX])
        T = sb("T", [P, 2, ROWS, TW], F16)
        Z = sb("Z", [W, (H + 2) * 2 * SLOT], F16)
        L0 = sb("L0", [P, BLOCKS, JROWS * W])
        Ls = sb("Ls", [P, JROWS * W])
        E = sb("E", [W, ROWS, NP])
        A = sb("A", [W, ROWS, NP])
        G = sb("G", [P, 2, ROWS * COLS])
        junk = sb("junk", [P, PIX], BF16)
        Wt = sb("Wt", [P, HALVES * PASSES, P], F16)
        A32 = sb("A32", [P, HALVES, 32])
        idf = sb("idf", [P, P])
        idh = sb("idh", [P, P], F16)
        gmat = sb("gmat", [P, P])
        par = sb("par", [P, 10, HALVES])
        dws = sb("dws", [P, HALVES, 9])
        pT = sb("pT", [P, HALVES, NP])
        vT = sb("vT", [P, HALVES, NP])
        mx = sb("mx", [W, ROWS])
        rs = sb("rs", [W, 2, ROWS])
        ysum = sb("ysum", [P, HALVES, BLOCKS * STRIPS])
        ysq = sb("ysq", [P, HALVES, BLOCKS * 2])
        tot = sb("tot", [P, 2, HALVES])
        gst = sb("gst", [P, 2, HALVES])
        aff = sb("aff", [P, 5, HALVES])
        neghalf = sb("neghalf", [P, HALVES])
        gs = sb("gs", [P, HALVES])
        gb = sb("gb", [P, HALVES])
        osc = sb("osc", [P, HALVES])
        bnw = sb("bnw", [P, 3, HALVES])
        mag = sb("mag", [P, 4, HALVES])
        l0c = sb("l0c", [P, 1])

        SL = HALVES * PIX
        posS = ring[:, 4 * SL:4 * SL + HALVES * POS * POS].rearrange("p (h y x) -> p h y x", h=HALVES, x=POS)
        spare = ring[:, 3 * SL:4 * SL]
        narrow = spare[:, 0:BLOCKS * JROWS * POS].rearrange("p (b y x) -> p b y x", b=BLOCKS, x=POS)
        sixth = spare[:, 2048:2048 + JROWS * POS].rearrange("p (y x) -> p y x", x=POS)
        half = spare[:, 3072:3072 + JROWS * POS // 2].rearrange("p (y x) -> p y x", x=POS // 2)
        K32 = spare[:, 4096:4096 + HALVES * P].rearrange("p (h n) -> p h n", h=HALVES)
        A3 = spare[:, 4608:4608 + 3 * HALVES * 32].rearrange("p (w h n) -> p w h n", w=3, h=HALVES)
        tail = ring[:, 5 * SL + 3072:6 * SL]
        wS = [tail[:, n * HALVES * C:(n + 1) * HALVES * C].rearrange("p (h n) -> p h n", h=HALVES) for n in range(4)]
        qwS, kwS, vwS, owS = wS
        Wf = G[:, 0, 0:HALVES * PASSES * P // 2].bitcast(F16).rearrange(
            "p (h q s c n) -> p h q s c n", h=HALVES, q=PASSES, s=4, c=2)
        CW = G[:, 1, 0:HALVES * 10 * NP].rearrange("p (h t n) -> p h t n", h=HALVES, n=NP)
        Whi = G[:, 1, 320:480].bitcast(F16).rearrange("p (h t n) -> p h t n", h=HALVES, n=NP)
        Wlo = G[:, 1, 480:640].bitcast(F16).rearrange("p (h t n) -> p h t n", h=HALVES, n=NP)

        conv_ps = ctx.enter_context(nc.psum_tensor("conv_ps", [P, 2, 2, 512], F32))
        out_ps = ctx.enter_context(nc.psum_tensor("out_ps", [P, 2, 512], F32))
        lg_ps = ctx.enter_context(nc.psum_tensor("lg_ps", [P, 512], F32))
        tr_ps = ctx.enter_context(nc.psum_tensor("tr_ps", [P, 512], F32))
        tr16 = tr_ps[:, :].bitcast(F16)
        pos_ps = [conv_ps[:, 1, 0, :], conv_ps[:, 1, 1, :], out_ps[:, 0, :]]

        small_in, weights_in, pos_in = sem("small_in"), sem("weights_in"), sem("pos_in")
        x_in = [[sem(f"x_in{k}a")] * 2 for k in range(RING)]
        for k in (0, BLOCKS):
            x_in[k] = [x_in[k][0], sem(f"x_in{k}b")]
        stored = [sem(f"stored{k}") for k in range(2 * UNITS)]
        pe_setup, vec_setup, act_setup, pool_setup = sem("pe_setup"), sem("vec_setup"), sem("act_setup"), sem("pool_setup")
        vec_step, pool_step = sem("vec_step"), sem("pool_step")
        conv_done, out_done = sem("conv_done"), sem("out_done")
        gelu_done = sem("gelu_done")
        out_added, y_done = sem("out_added"), sem("y_done")
        lg_done, lg_copied = sem("lg_done"), sem("lg_copied")
        t1_done, max_done, sub_done = sem("t1_done"), sem("max_done"), sem("sub_done")
        exp_done, soft_step, probs_ready = sem("exp_done"), sem("soft_step"), sem("probs_ready")
        t2_done, t2_copied = sem("t2_done"), sem("t2_copied")
        sq_done = sem("sq_done")
        tot_done, group_done, group_copied = sem("tot_done"), sem("group_done"), sem("group_copied")
        norm_done = sem("norm_done")

        PE_KV, PE_A, PE_POS, PE_WT = 1, 2, 3, 3 + BLOCKS
        VEC_KV, VEC_A, VEC_WF, VEC_WT, VEC_L0 = range(1, 6)

        def until(eng, semaphore, value):
            if not isinstance(value, int) or value > 0:
                eng.wait_ge(semaphore, value)

        def halves(k):
            return ring[:, k * SL:(k + 1) * SL].rearrange("p (h y x) -> p h y x", h=HALVES, x=W)

        def place(j, u):
            r0, n, h = SPANS[u]
            return halves(j * BLOCKS + r0 // ROWS)[:, h, r0 % ROWS:r0 % ROWS + n, :].rearrange("p y x -> p (y x)")

        def passes(eng, body):
            body(0)
            with eng.Fori(1, PAIRS - 1) as i:
                body(i)
            body(PAIRS - 1)

        def fronted(t):
            return not isinstance(t, int) or t < LAST

        block = ctx.enter_context(nc.Block())

        @block.sync
        def _(sp):
            def unit(dram, b, u):
                r0, n, h = SPANS[u]
                return dram[b, h * P:(h + 1) * P, r0:r0 + n, :].rearrange("c y x -> c (y x)")

            def load(b, j, u):
                r0 = SPANS[u][0]
                arrived = x_in[j * BLOCKS + r0 // ROWS][r0 % ROWS // HROWS]
                sp.dma_start(place(j, u), unit(x, b, u)).then_inc(arrived, 16)

            sp.dma_start(par[:, :, :], params).then_inc(small_in, 16)
            sp.dma_start(pT[:, :, :], protoT.rearrange("(h p) n -> p h n", p=P)).then_inc(small_in, 16)
            for dst, src in ((kwS, kwT), (vwS, vwT), (qwS, qw), (owS, owT)):
                sp.dma_start(dst, src.rearrange("(h p) n -> p h n", p=P)).then_inc(weights_in, 16)
            sp.dma_start(dws[:, :, :], dw).then_inc(small_in, 16)
            sp.dma_start(idf[:, :], ident).then_inc(small_in, 16)
            sp.dma_start(gmat[:, :], group_mean).then_inc(small_in, 16)
            sp.dma_start(posS.rearrange("p h y x -> p h (y x)"), pos.rearrange("(h p) n -> p h n", p=P)).then_inc(pos_in, 16)
            for u in range(UNITS):
                load(0, 0, u)
            sp.wait_ge(vec_setup, VEC_L0)
            for u in range(UNITS):
                load(1, 1, u)

            ORDER = [("store", 0), ("store", 1), ("load", 0), ("load", 1), ("store", 2), ("store", 3), ("load", 2)]
            for u in range(4, UNITS):
                ORDER += [("store", u), ("load", u - 1)]
            ORDER += [("load", UNITS - 1)]

            def store_and_reload(i, j, reload):
                for what, u in ORDER:
                    if what == "store":
                        until(sp, norm_done, UNITS * (2 * i + j) + u + 1)
                        sp.dma_start(unit(out, 2 * i + j, u), place(j, u)).then_inc(stored[j * UNITS + u], 16)
                    elif reload:
                        until(sp, stored[j * UNITS + u], 16 * (i + 1))
                        load(2 * i + j + 2, j, u)

            store_and_reload(0, 0, True)
            with sp.Fori(1, PAIRS - 1) as i:
                store_and_reload(i - 1, 1, True)
                store_and_reload(i, 0, True)
            store_and_reload(PAIRS - 2, 1, True)
            store_and_reload(PAIRS - 1, 0, False)
            store_and_reload(PAIRS - 1, 1, False)
            for u in range(2 * UNITS):
                sp.wait_ge(stored[u], 16 * PAIRS)

        @block.gpsimd
        def _(pool):
            nc.gpsimd.memset(K32, 0.0)
            nc.gpsimd.memset(A32[:, :, :], 0.0)
            nc.gpsimd.memset(Wf, 0.0)
            nc.gpsimd.memset(ysq[:, :, :], 0.0)
            nc.gpsimd.memset(neghalf[:, :], -0.5).then_inc(pool_setup, 1)
            nc.gpsimd.memset(Z[:, 0:2 * SLOT], 0.0)
            nc.gpsimd.memset(Z[:, (H + 1) * 2 * SLOT:(H + 2) * 2 * SLOT], 0.0)
            for k in range(2):
                nc.gpsimd.memset(T[:, k, :, 0:2], 0.0)
                nc.gpsimd.memset(T[:, k, :, TW - 2:TW], 0.0)
            pool.wait_ge(small_in, 80)
            nc.gpsimd.tensor_scalar(bnw[:, 0, :], par[:, BN_VAR, :], EPS, None, ALU.add).then_inc(pool_step, 1)
            pool.wait_ge(pool_step, 1)
            pool.wait_ge(pool_setup, 1)
            nc.gpsimd.tensor_tensor(bnw[:, 1, :], bnw[:, 0, :], neghalf[:, :], ALU.pow).then_inc(pool_step, 1)
            pool.wait_ge(pool_step, 2)
            nc.gpsimd.tensor_tensor(bnw[:, 2, :], bnw[:, 1, :], par[:, BN_G, :], ALU.mult).then_inc(pool_setup, 1)

            def normalise(b, j):
                until(pool, group_copied, b + 1)
                mean, msq = gst[:, 0, :], gst[:, 1, :]

                def step(n, inst):
                    pool.drain()

                step(0, nc.gpsimd.tensor_tensor(aff[:, 0, :], mean, mean, ALU.mult))
                step(1, nc.gpsimd.tensor_tensor(aff[:, 0, :], msq, aff[:, 0, :], ALU.subtract))
                step(2, nc.gpsimd.tensor_scalar(aff[:, 0, :], aff[:, 0, :], 0.0, EPS, ALU.max, ALU.add))
                step(3, nc.gpsimd.tensor_tensor(aff[:, 1, :], aff[:, 0, :], neghalf[:, :], ALU.pow))
                step(4, nc.gpsimd.tensor_tensor(aff[:, 2, :], aff[:, 1, :], par[:, GN_G, :], ALU.mult))
                step(5, nc.gpsimd.tensor_tensor(aff[:, 3, :], aff[:, 2, :], mean, ALU.mult))
                step(6, nc.gpsimd.tensor_tensor(aff[:, 4, :], par[:, GN_B, :], aff[:, 3, :], ALU.subtract))
                for u in range(UNITS):
                    h = SPANS[u][2]
                    at_u = place(j, u)
                    nc.gpsimd.tensor_scalar(at_u, at_u, aff[:, 2, h:h + 1], aff[:, 4, h:h + 1],
                                            ALU.mult, ALU.add).then_inc(norm_done, 1)

            normalise(0, 0)
            with pool.Fori(1, PAIRS - 1) as i:
                normalise(2 * i - 1, 1)
                normalise(2 * i, 0)
            for b in (B - 3, B - 2, B - 1):
                normalise(b, b % 2)

        @block.tensor
        def _(pe):
            small = conv_ps[:, 0, 0, :]
            pe.wait_ge(small_in, 80)
            pe.wait_ge(weights_in, 64)
            for n, w in enumerate((kwS, vwS)):
                for dh in range(HALVES):
                    for ch in range(HALVES):
                        last = nc.tensor.matmul(small[:, (2 * n + dh) * NP:(2 * n + dh + 1) * NP],
                                                w[:, ch, dh * P:(dh + 1) * P], pT[:, ch, :],
                                                start=ch == 0, stop=ch == HALVES - 1)
            last.then_inc(pe_setup, 1)
            pe.wait_ge(vec_setup, VEC_KV)
            second = conv_ps[:, 0, 1, :]
            for n, (w, r) in enumerate(((qwS, K32), (owS, vT))):
                for ch in range(HALVES):
                    for dh in range(HALVES):
                        nc.tensor.matmul(second[:, (2 * n + ch) * NP:(2 * n + ch + 1) * NP],
                                         w[:, dh, ch * P:(ch + 1) * P], r[:, dh, 0:NP],
                                         start=dh == 0, stop=dh == HALVES - 1)
            for dh in range(HALVES):
                last = nc.tensor.matmul(second[:, 64:65], K32[:, dh, :], par[:, Q_B, dh:dh + 1],
                                        start=dh == 0, stop=dh == HALVES - 1)
            last.then_inc(pe_setup, 1)
            TAPS = [[(0, 5 / 6), (-1, 1 / 6)], [(0, 1 / 2), (1, 1 / 2)], [(1, 5 / 6), (2, 1 / 6)]]
            SCALED = {1 / 6: 0, 5 / 6: 1, 1 / 2: 2}

            def resized_rows(kb, g, j):
                first = kb * ROWS + g * HROWS + j * (JROWS // 2)
                for phase in range(3):
                    ys = [y for y in range(first, first + JROWS // 2) if y % 3 == phase]
                    terms = [(ys, [min(max(2 * (y // 3) + d, 0), POS - 1) for y in ys], scale, ch)
                             for d, scale in TAPS[phase] for ch in range(HALVES)]
                    for n, (ys, src, scale, ch) in enumerate(terms):
                        step = src[1] - src[0] if len(src) > 1 else 1
                        yield (slice(ys[0] - first + g * 4, ys[-1] - first + g * 4 + 1, 3), slice(src[0], src[-1] + 1, step),
                               SCALED[scale], ch, n == 0, n == len(terms) - 1)

            pe.wait_ge(vec_setup, VEC_A)
            pe.wait_ge(pos_in, 16)
            for kb in range(BLOCKS):
                for g in range(2):
                    for tiles in zip(*(resized_rows(kb, g, j) for j in range(JT))):
                        for j, (ys, src, scale, ch, first, final) in enumerate(tiles):
                            last = nc.tensor.matmul(
                                pos_ps[kb][32 * j:32 * j + 32, :].rearrange("p (y x) -> p y x", x=POS)[:, ys, :],
                                A3[:, scale, ch, :], posS[:, ch, src, :], start=first, stop=final)
                last.then_inc(pe_setup, 1)
            pe.wait_ge(vec_setup, VEC_WF)
            for h in range(HALVES):
                turned = conv_ps[:, 0, h, :].bitcast(F16)
                for q in range(PASSES):
                    last = nc.tensor.transpose(turned[:, q * P:(q + 1) * P],
                                               Wf[:, h, q].rearrange("p s c n -> p (s c n)"), idh[:, :])
            last.then_inc(pe_setup, 1)

            def logits(m, pair, k, g):
                until(pe, x_in[k][g], 32 * (pair + 1))
                until(pe, sub_done, 2 * m + g)
                xs = halves(k)
                for ch in range(HALVES):
                    for j in range(JT):
                        r0 = g * HROWS + j * (JROWS // 2)
                        last = nc.tensor.matmul(lg_ps[32 * j:32 * j + 32, 0:JROWS // 2 * W], A32[:, ch, 0:32],
                                                xs[:, ch, r0:r0 + JROWS // 2, :],
                                                start=ch == 0, stop=ch == HALVES - 1)
                last.then_inc(lg_done, 1)

            def turn_logits(m, g):
                until(pe, lg_copied, 2 * m + g + 1)
                for i in range(JROWS // 2):
                    r = g * (JROWS // 2) + i
                    last = nc.tensor.transpose(lg_ps[0:W, i * P:(i + 1) * P], Ls[:, r * W:(r + 1) * W], idf[:, :])
                last.then_inc(t1_done, 1)

            def turn_probs(t, kb, g):
                if g == T2G - 1 and kb < BLOCKS - 1:
                    until(pe, probs_ready, t + 2)
                elif g == 0:
                    until(pe, probs_ready, t + 1)
                until(pe, t2_copied, T2G * t + g)
                for r in range(ROWS // T2G):
                    y = kb * ROWS + g * (ROWS // T2G) + r
                    last = nc.tensor.transpose(tr16[:, r * W:(r + 1) * W],
                                               Z[:, (2 * y + 1) * SLOT:(2 * y + 1) * SLOT + 4 * SLOT], idh[0:W, 0:W])
                last.then_inc(t2_done, 1)

            def group_means(b):
                until(pe, tot_done, 2 * (b + 1))
                nc.tensor.matmul(tr_ps[:, 0:2 * HALVES], gmat[:, :], tot[:, :, :].rearrange("p a h -> p (a h)"),
                                 start=True, stop=True).then_inc(group_done, 1)

            def conv_half(n, h, s, buf, row_half):
                for dx in range(3):
                    for part in range(2):
                        last = nc.tensor.matmul(
                            conv_ps[:, n % 2, row_half, :], Wt[:, h * PASSES + 2 * dx + part, :],
                            T[:, buf, row_half * 16:row_half * 16 + 16, 1 + s * COLS + dx:1 + s * COLS + dx + COLS],
                            start=dx == 0 and part == 0, stop=dx == 2 and part == 1)
                return last

            pe.wait_ge(vec_setup, VEC_L0)
            pe.wait_ge(vec_setup, VEC_WT)
            for m in range(2):
                for g in range(2):
                    logits(m, 0, m, g)
                    turn_logits(m, g)
            pe.wait_ge(pool_setup, 2)
            for g in range(T2G):
                turn_probs(0, 0, g)

            def body(i):
                for k in range(RING):
                    t, kb, m, mk = RING * i + k, k % BLOCKS, RING * i + k + 2, (k + 2) % RING
                    image_ended = kb == 0 and not (isinstance(t, int) and t == 0)
                    for n in range(TILES):
                        h, s = divmod(n, STRIPS)
                        at = TILES * t + n
                        if n == 0:
                            until(pe, t2_copied, T2G * t + 2)
                        until(pe, gelu_done, at - 1)
                        conv_half(n, h, s, k % 2, 0)
                        if n == 0 and fronted(m):
                            logits(m, i + (k + 2) // RING, mk, 0)
                        if n == 1 and fronted(m):
                            turn_logits(m, 0)
                        if n == 1 and fronted(t + 1):
                            if image_ended:
                                until(pe, group_copied, 2 * i + k // BLOCKS)
                            turn_probs(t + 1, (k + 1) % BLOCKS, 0)
                        if n == 0:
                            until(pe, t2_copied, T2G * (t + 1))
                        conv_half(n, h, s, k % 2, 1).then_inc(conv_done, 1)
                        until(pe, out_added, at)
                        for row_half in range(2):
                            last = nc.tensor.matmul(
                                out_ps[:, row_half, :], Wt[:, h * PASSES + PASSES - 1, :],
                                T[:, k % 2, row_half * 16:row_half * 16 + 16, 2 + s * COLS:2 + s * COLS + COLS],
                                start=True, stop=True)
                        last.then_inc(out_done, 1)
                        if n == 1 and fronted(m):
                            logits(m, i + (k + 2) // RING, mk, 1)
                        if n == 2 and fronted(m):
                            turn_logits(m, 1)
                        if n == 0 and image_ended:
                            group_means(2 * i + k // BLOCKS - 1)
                        if fronted(t + 1):
                            if n in (2, 3, 5):
                                turn_probs(t + 1, (k + 1) % BLOCKS, (n + 1) // 2)

            passes(pe, body)
            group_means(B - 1)

        @block.scalar
        def _(act):
            act.wait_ge(vec_setup, VEC_A)
            for kb in range(BLOCKS):
                act.wait_ge(pe_setup, PE_POS + kb)
                nc.scalar.activation(narrow[:, kb].rearrange("p y x -> p (y x)"), pos_ps[kb], ACT.Identity,
                                     bias=l0c[:, :]).then_inc(act_setup, 1)
            act.wait_ge(vec_setup, VEC_L0)
            act.wait_ge(pool_setup, 2)

            def exponent(m):
                act.wait_ge(sub_done, 2 * m + 2)
                nc.scalar.activation(E[:, :, :], E[:, :, :], ACT.Exp).then_inc(exp_done, 1)

            def copy_probs(t, buf, g):
                if g == 0:
                    until(act, out_done, TILES * (t - 1))
                act.wait_ge(t2_done, T2G * t + g + 1)
                nc.scalar.activation(T[:, buf, g * 8:(g + 1) * 8, 2:2 + W],
                                     tr16[:, 0:8 * W].rearrange("p (y x) -> p y x", x=W), ACT.Copy)\
                    .then_inc(t2_copied, 1)

            def square(k, h, c0, c1, slot, count, before):
                act.wait_ge(y_done, count)
                until(act, sq_done, before)
                src = halves(k)[:, h, :, c0:c1]
                nc.scalar.activation(junk[:, 0:ROWS * (c1 - c0)].rearrange("p (y x) -> p y x", y=ROWS), src, ACT.Square,
                                     accum_out=ysq[:, h, (k % BLOCKS) * 2 + slot:(k % BLOCKS) * 2 + slot + 1])\
                    .then_inc(sq_done, 1)

            exponent(0)
            exponent(1)
            for g in range(T2G):
                copy_probs(0, 0, g)

            def body(i):
                for k in range(RING):
                    t = RING * i + k
                    for n in range(TILES):
                        h, s = divmod(n, STRIPS)
                        at = TILES * t + n
                        if n == 0 and not (isinstance(t, int) and t == 0):
                            square((k - 1) % RING, 1, 2 * COLS, W, 1, TILES * t, 3 * t - 1)
                        if n == 3 and fronted(t + 2):
                            exponent(t + 2)
                        if n == 1 and fronted(t + 1):
                            copy_probs(t + 1, (k + 1) % 2, 0)
                        act.wait_ge(conv_done, at + 1)
                        until(act, y_done, at - 1)
                        nc.scalar.activation(G[:, n % 2, :], conv_ps[:, n % 2, :, :].rearrange("p a b -> p (a b)"),
                                             ACT.Gelu, bias=gb[:, h:h + 1], scale=gs[:, h:h + 1])\
                            .then_inc(gelu_done, 1)
                        if fronted(t + 1):
                            if n in (2, 3, 5):
                                copy_probs(t + 1, (k + 1) % 2, (n + 1) // 2)
                        if n == 4:
                            square(k, 0, 0, W, 0, TILES * t + 3, 3 * t)
                        if n == 5:
                            square(k, 1, 0, 2 * COLS, 0, TILES * t + 5, 3 * t + 1)

            passes(act, body)
            square(RING - 1, 1, 2 * COLS, W, 1, TILES * LAST, 3 * LAST - 1)

        @block.vector
        def _(dve):
            count = [0]

            def step(inst):
                count[0] += 1
                inst.then_inc(vec_step, 1)
                dve.wait_ge(vec_step, count[0])

            small = conv_ps[:, 0, 0, :]
            second = conv_ps[:, 0, 1, :]
            dve.wait_ge(small_in, 80)
            dve.wait_ge(pool_setup, 1)
            nc.vector.tensor_copy(idh[:, :], idf[:, :])
            dve.wait_ge(pe_setup, PE_KV)
            for dh in range(HALVES):
                nc.vector.tensor_scalar(K32[:, dh, :].rearrange("p (j n) -> p j n", n=32)[:, :, 0:NP],
                                        small[:, dh * NP:(dh + 1) * NP].unsqueeze(1).to_broadcast([P, JT, NP]),
                                        par[:, K_B, dh:dh + 1], C ** -0.5, ALU.add, ALU.mult)
                last = nc.vector.tensor_scalar(vT[:, dh, :], small[:, (2 + dh) * NP:(3 + dh) * NP],
                                               par[:, V_B, dh:dh + 1], None, ALU.add)
            last.then_inc(vec_setup, 1)
            dve.wait_ge(pe_setup, PE_A)
            nc.vector.tensor_copy(l0c[:, :], second[:, 64:65])
            made = second[:, 0:HALVES * NP].rearrange("p (h n) -> p h n", h=HALVES)
            step(nc.vector.tensor_copy(A32[:, :, 0:NP], made))
            for n, scale in enumerate((1 / 6, 5 / 6, 1 / 2)):
                last = nc.vector.tensor_scalar(A3[:, n], A32[:, :, :], scale, None, ALU.mult)
            last.then_inc(vec_setup, 1)

            for h in range(HALVES):
                last = nc.vector.tensor_scalar(CW[:, h, 9, :], second[:, (2 + h) * NP:(3 + h) * NP],
                                               par[:, OUT_B, h:h + 1], None, ALU.add)
            step(last)
            for h in range(HALVES):
                last = nc.vector.tensor_tensor(CW[:, h, 0:9, :], CW[:, h, 9:10, :].to_broadcast([P, 9, NP]),
                                               dws[:, h, :].unsqueeze(2).to_broadcast([P, 9, NP]), ALU.mult)
            step(last)
            nc.vector.tensor_reduce(mag[:, 0, :], CW[:, :, 0:9, :].rearrange("p h t n -> p h (t n)"), AX, ALU.max,
                                    apply_absolute_value=True)
            step(nc.vector.tensor_reduce(mag[:, 1, :], CW[:, :, 9, :], AX, ALU.max, apply_absolute_value=True))
            step(nc.vector.tensor_scalar(mag[:, 0:2, :], mag[:, 0:2, :], 1e-30, None, ALU.max))
            step(nc.vector.tensor_scalar(mag[:, 0:2, :].bitcast(I32), mag[:, 0:2, :].bitcast(I32), 0x7F800000, None,
                                         ALU.bitwise_and))
            step(nc.vector.reciprocal(mag[:, 2:4, :], mag[:, 0:2, :]))
            for h in range(HALVES):
                nc.vector.tensor_scalar(CW[:, h, 0:9, :], CW[:, h, 0:9, :], mag[:, 2, h:h + 1], WT_SCALE,
                                        ALU.mult, ALU.mult)
                last = nc.vector.tensor_scalar(CW[:, h, 9, :], CW[:, h, 9, :], mag[:, 3, h:h + 1], WT_SCALE,
                                               ALU.mult, ALU.mult)
            step(last)
            step(nc.vector.tensor_copy(Whi, CW))
            step(nc.vector.tensor_tensor(Wlo, CW, Whi, ALU.subtract))
            for h in range(HALVES):
                def fill(q, slot, src, tap):
                    return nc.vector.tensor_copy(Wf[:, h, q, slot], src[:, h, tap:tap + 1, :].to_broadcast([P, 2, NP]))
                for dx in range(3):
                    fill(2 * dx, 0, Whi, dx)
                    fill(2 * dx, 1, Whi, 3 + dx)
                    fill(2 * dx, 2, Wlo, 3 + dx)
                    fill(2 * dx, 3, Whi, 6 + dx)
                    fill(2 * dx + 1, 0, Wlo, dx)
                    fill(2 * dx + 1, 3, Wlo, 6 + dx)
                fill(PASSES - 1, 1, Whi, 9)
                last = fill(PASSES - 1, 2, Wlo, 9)
            last.then_inc(vec_setup, 1)
            dve.wait_ge(pool_setup, 2)
            step(nc.vector.tensor_tensor(gb[:, :], par[:, BN_MEAN, :], bnw[:, 2, :], ALU.mult))
            nc.vector.tensor_tensor(gb[:, :], par[:, BN_B, :], gb[:, :], ALU.subtract)
            step(nc.vector.tensor_tensor(gs[:, :], mag[:, 0, :], bnw[:, 2, :], ALU.mult))
            nc.vector.tensor_scalar(gs[:, :], gs[:, :], UNSCALE, None, ALU.mult)
            nc.vector.tensor_scalar(osc[:, :], mag[:, 1, :], UNSCALE, None, ALU.mult)
            dve.wait_ge(pe_setup, PE_WT)
            for h in range(HALVES):
                last = nc.vector.tensor_copy(Wt[:, h * PASSES:(h + 1) * PASSES, :].rearrange("p q c -> p (q c)"),
                                             conv_ps[:, 0, h, :].bitcast(F16)[:, 0:PASSES * P])
            last.then_inc(vec_setup, 1)

            def mix(o, whole, part, by):
                return nc.vector.scalar_tensor_tensor(out=o, in0=whole, scalar=by, in1=part, op0=ALU.mult, op1=ALU.add)

            for kb in range(BLOCKS):
                src, dst = narrow[:, kb], L0[:, kb, :].rearrange("p (y x) -> p y x", x=W)
                dve.wait_ge(act_setup, kb + 1)
                nc.vector.tensor_copy(dst[:, :, 0:1], src[:, :, 0:1])
                nc.vector.tensor_copy(dst[:, :, W - 1:W], src[:, :, POS - 1:POS])
                step(nc.vector.tensor_scalar(sixth, src, 1 / 6, None, ALU.mult))
                step(nc.vector.tensor_scalar(half, src[:, :, 1::2], 1 / 2, None, ALU.mult))
                mix(dst[:, :, 3::3], src[:, :, 2::2], sixth[:, :, 1:POS - 1:2], 5 / 6)
                mix(dst[:, :, 1::3], src[:, :, 0::2], half, 1 / 2)
                last = mix(dst[:, :, 2:W - 1:3], src[:, :, 1:POS - 1:2], sixth[:, :, 2::2], 5 / 6)
                if kb < BLOCKS - 1:
                    step(last)
            last.then_inc(vec_setup, 1)
            dve.wait_ge(vec_setup, VEC_L0)

            HALF = JROWS // 2 * W

            def add_l0(m, kb, g):
                dve.wait_ge(lg_done, 2 * m + g + 1)
                until(dve, t1_done, 2 * m + g - 1)
                nc.vector.tensor_tensor(Ls[:, g * HALF:(g + 1) * HALF], lg_ps[:, 0:HALF],
                                        L0[:, kb, g * HALF:(g + 1) * HALF], ALU.add).then_inc(lg_copied, 1)

            def subtract_max(m, g):
                dve.wait_ge(t1_done, 2 * m + g + 1)
                lg = lg_ps[0:W, :].rearrange("x (i j n) -> x i j n", i=JROWS // 2, n=32)[:, :, :, 0:NP]
                most = mx[:, g * 16:(g + 1) * 16].rearrange("x (i j) -> x i j", j=JT)
                nc.vector.tensor_reduce(most, lg, AX, ALU.max).then_inc(max_done, 1)
                dve.wait_ge(max_done, 2 * m + g + 1)
                dst = E[:, g * HROWS:(g + 1) * HROWS, :].rearrange("x (j i) n -> x i j n", j=JT)
                nc.vector.tensor_tensor(dst, lg, most.unsqueeze(3).to_broadcast([W, JROWS // 2, JT, NP]),
                                        ALU.subtract).then_inc(sub_done, 1)

            SOFT = 5

            def chain(m, n, inst):
                inst.then_inc(soft_step, 1)
                dve.wait_ge(soft_step, SOFT * m + n + 1)

            def probabilities(m):
                dve.wait_ge(exp_done, m + 1)
                chain(m, 0, nc.vector.tensor_reduce(rs[:, 0, :], E[:, :, :], AX, ALU.add))
                chain(m, 1, nc.vector.reciprocal(rs[:, 1, :], rs[:, 0, :]))
                chain(m, 2, nc.vector.scalar_tensor_tensor(out=A[:, :, :], in0=E[:, :, :], scalar=PROB_SCALE,
                                                           in1=rs[:, 1, :].unsqueeze(2).to_broadcast([W, ROWS, NP]),
                                                           op0=ALU.mult, op1=ALU.mult))

            def split_probs(m, kb):
                r0 = 1 + kb * ROWS
                z = Z[:, r0 * 2 * SLOT:(r0 + ROWS) * 2 * SLOT].rearrange("x (y d c n) -> x y d c n", d=2, c=2, n=NP)
                until(dve, t2_done, T2G * (m - 2))
                chain(m, 3, nc.vector.tensor_copy(z[:, :, 0, 0, :], A[:, :, :]))
                chain(m, 4, nc.vector.tensor_tensor(z[:, :, 0, 1, :], A[:, :, :], z[:, :, 0, 0, :], ALU.subtract))
                zz = Z[:, r0 * 2 * SLOT:(r0 + ROWS) * 2 * SLOT].rearrange("x (y d n) -> x y d n", d=2, n=SLOT)
                nc.vector.tensor_copy(zz[:, :, 1, :], zz[:, :, 0, :]).then_inc(probs_ready, 1)

            def add_out(k, n, at):
                h, s = divmod(n, STRIPS)
                dve.wait_ge(out_done, at + 1)
                v = halves(k)[:, h, :, s * COLS:(s + 1) * COLS]
                nc.vector.scalar_tensor_tensor(out=v, in0=out_ps[:, :, :].rearrange("p a (y x) -> p (a y) x", x=COLS),
                                               scalar=osc[:, h:h + 1], in1=v, op0=ALU.mult, op1=ALU.add)\
                    .then_inc(out_added, 1)

            def add_gelu(k, n, at):
                h, s = divmod(n, STRIPS)
                dve.wait_ge(gelu_done, at + 1)
                dve.wait_ge(out_added, at + 1)
                v = halves(k)[:, h, :, s * COLS:(s + 1) * COLS]
                c = (k % BLOCKS) * STRIPS + s
                nc.vector.scalar_tensor_tensor(out=v, in0=G[:, n % 2, :].rearrange("p (y x) -> p y x", x=COLS), scalar=1.0,
                                               in1=v, op0=ALU.mult, op1=ALU.add, accum_out=ysum[:, h, c:c + 1])\
                    .then_inc(y_done, 1)

            def sum_image(t, b):
                dve.wait_ge(sq_done, 3 * t)
                dve.wait_ge(y_done, TILES * t)
                nc.vector.tensor_reduce(tot[:, 0, :], ysum[:, :, :], AX, ALU.add).then_inc(tot_done, 1)
                nc.vector.tensor_reduce(tot[:, 1, :], ysq[:, :, :], AX, ALU.add).then_inc(tot_done, 1)
                dve.wait_ge(tot_done, 2 * (b + 1))

            def take_means(b):
                dve.wait_ge(group_done, b + 1)
                until(dve, norm_done, UNITS * (b - 1) + 1)
                nc.vector.tensor_copy(gst[:, :, :].rearrange("p a h -> p (a h)"), tr_ps[:, 0:2 * HALVES])\
                    .then_inc(group_copied, 1)

            for m in range(2):
                for g in range(2):
                    add_l0(m, m, g)
                    subtract_max(m, g)
                probabilities(m)
                split_probs(m, m)

            def body(i):
                for k in range(RING):
                    t, m = RING * i + k, RING * i + k + 2
                    mb = (k + 2) % BLOCKS
                    b = 2 * i + k // BLOCKS - 1
                    image_ended = k % BLOCKS == 0 and not (isinstance(t, int) and t == 0)
                    for n in range(TILES):
                        at = TILES * t + n
                        if n == 1 and image_ended:
                            take_means(b)
                        if n == 4 and fronted(m):
                            probabilities(m)
                        if n == 5 and fronted(m):
                            split_probs(m, mb)
                        if not (n == 0 and isinstance(t, int) and t == 0):
                            add_gelu((k - (n == 0)) % RING, (n - 1) % TILES, at - 1)
                        if fronted(m):
                            if n == 0:
                                add_l0(m, mb, 0)
                            if n == 1:
                                subtract_max(m, 0)
                            if n == 2:
                                add_l0(m, mb, 1)
                            if n == 3:
                                subtract_max(m, 1)
                        if n == 0 and image_ended:
                            sum_image(t, b)
                        add_out(k, n, at)

            passes(dve, body)
            add_gelu(RING - 1, TILES - 1, TILES * LAST - 1)
            sum_image(LAST, B - 1)
            take_means(B - 1)


def kernel(**inputs):
    import concourse.bacc as bacc
    from concourse.bass_utils import run_bass_kernel_spmd

    a = {k.removeprefix("L0_conv_"): np.asarray(v) for k, v in inputs.items()}
    vectors = np.stack([a[n] for n in ("q_b", "k_b", "v_b", "out_b", "bn_g", "bn_b", "bn_mean", "bn_var", "gn_g", "gn_b")])
    same_group = np.kron(np.eye(P // GROUP), np.ones((GROUP, GROUP)))
    arrays = {
        "x": a["x"],
        "params": vectors.reshape(10, HALVES, P).transpose(2, 0, 1),
        "dw": a["dw_w"].reshape(HALVES, P, 9).transpose(1, 0, 2),
        "qw": a["q_w"],
        "kwT": a["k_w"].T,
        "vwT": a["v_w"].T,
        "owT": a["out_w"].T,
        "protoT": a["prototypes"][0].T,
        "pos": a["pos_embed"].reshape(C, POS * POS),
        "ident": np.eye(P, dtype=np.float32),
        "group_mean": (same_group / (GROUP * H * W)).astype(np.float32),
    }
    arrays = {f"in_{k}": np.ascontiguousarray(v) for k, v in arrays.items()}
    nc = bacc.Bacc("TRN2", target_bir_lowering=False, num_devices=1)
    args = [nc.dram_tensor(k, v.shape, mybir.dt.from_np(v.dtype), kind="ExternalInput").ap() for k, v in arrays.items()]
    out = nc.dram_tensor("out", (B, C, H, W), F32, kind="ExternalOutput").ap()
    build(nc, *args, out)
    r = run_bass_kernel_spmd(nc, [arrays], core_ids=[0])
    return r.results[0]["out"]
```

```python
from contextlib import ExitStack

import numpy as np

import concourse.bass as bass
from concourse import mybir

F32 = mybir.dt.float32
F16 = mybir.dt.float16
BF16 = mybir.dt.bfloat16
I32 = mybir.dt.int32
ALU = mybir.AluOpType
ACT = mybir.ActivationFunctionType
AX = mybir.AxisListType.X

B, C, H, W = 16, 256, 96, 96
NP = 16
POS = 64
P = 128
HALVES = C // P
GROUP = C // 8
EPS = 1e-5
ROWS = 32
COLS = 32
BLOCKS = H // ROWS
STRIPS = W // COLS
TILES = HALVES * STRIPS
PIX = ROWS * W
RING = 2 * BLOCKS
PAIRS = B // 2
LAST = B * BLOCKS
HROWS = ROWS // 2
SPANS = [(y, HROWS, h) for y in range(0, H, HROWS) for h in range(HALVES)]
UNITS = len(SPANS)
STEPS = UNITS // HALVES
JT = 4
JROWS = ROWS // JT
ZROW = 3 * NP
TW = W + 4
GROUPS = [(-1, 9), (8, 8), (16, 8), (24, 7), (31, 1)]
T2G = len(GROUPS)
PROB_SCALE = 1024.0
WT_SCALE = 256.0
UNSCALE = 1.0 / (PROB_SCALE * WT_SCALE)
LOW, PLAIN = 3, 4
PASSES = 5

Q_B, K_B, V_B, OUT_B, BN_G, BN_B, BN_MEAN, BN_VAR, GN_G, GN_B = range(10)


def build(nc, x, params, dw, qw, kwT, vwT, owT, protoT, pos, ident, group_mean, out):
    ctx = ExitStack()
    with ctx:
        def sb(name, shape, dt=F32):
            return ctx.enter_context(nc.sbuf_tensor(name, shape, dt))

        def sem(name):
            return ctx.enter_context(nc.semaphore(name))

        ring = sb("ring", [P, RING * HALVES * PIX])
        T = sb("T", [P, 2, ROWS + 1, TW], F16)
        Tlow = sb("Tlow", [P, 2, ROWS * TW], F16)
        Z = sb("Z", [W, (H + 3) * ZROW], F16)
        L0 = sb("L0", [P, BLOCKS, JROWS * W])
        Ls = sb("Ls", [P, JROWS // 2 * W])
        E = sb("E", [W, ROWS, NP])
        G = sb("G", [P, 2, ROWS * COLS])
        junk = sb("junk", [P, ROWS * COLS], BF16)
        Wt = sb("Wt", [P, HALVES * PASSES, P], F16)
        A32 = sb("A32", [P, HALVES, 32])
        idf = sb("idf", [P, P])
        idh = sb("idh", [P, P], F16)
        gmat = sb("gmat", [P, P])
        par = sb("par", [P, 10, HALVES])
        dws = sb("dws", [P, HALVES, 9])
        pT = sb("pT", [P, HALVES, NP])
        vT = sb("vT", [P, HALVES, NP])
        mx = sb("mx", [W, ROWS])
        rs = sb("rs", [W, 2, ROWS])
        ystat = sb("ystat", [P, 2, HALVES, BLOCKS * STRIPS])
        tot = sb("tot", [P, 2, HALVES])
        gst = sb("gst", [P, 2, HALVES])
        aff = sb("aff", [P, 5, HALVES])
        neghalf = sb("neghalf", [P, HALVES])
        warm = sb("warm", [P, HALVES])
        gs = sb("gs", [P, HALVES])
        gb = sb("gb", [P, HALVES])
        osc = sb("osc", [P, HALVES])
        bnw = sb("bnw", [P, 3, HALVES])
        mag = sb("mag", [P, 4, HALVES])
        l0c = sb("l0c", [P, 1])

        SL = HALVES * PIX
        posS = ring[:, 4 * SL:4 * SL + HALVES * POS * POS].rearrange("p (h y x) -> p h y x", h=HALVES, x=POS)
        spare = ring[:, 3 * SL:4 * SL]
        narrow = spare[:, 0:BLOCKS * JROWS * POS].rearrange("p (b y x) -> p b y x", b=BLOCKS, x=POS)
        sixth = spare[:, 2048:2048 + JROWS * POS].rearrange("p (y x) -> p y x", x=POS)
        half = spare[:, 3072:3072 + JROWS * POS // 2].rearrange("p (y x) -> p y x", x=POS // 2)
        K32 = spare[:, 4096:4096 + HALVES * P].rearrange("p (h n) -> p h n", h=HALVES)
        A3 = spare[:, 4608:4608 + 3 * HALVES * 32].rearrange("p (w h n) -> p w h n", w=3, h=HALVES)
        tail = ring[:, 5 * SL + 3072:6 * SL]
        wS = [tail[:, n * HALVES * C:(n + 1) * HALVES * C].rearrange("p (h n) -> p h n", h=HALVES) for n in range(4)]
        qwS, kwS, vwS, owS = wS
        Wf = G[:, 0, 0:HALVES * PASSES * P // 2].bitcast(F16).rearrange(
            "p (h q s n) -> p h q s n", h=HALVES, q=PASSES, n=NP)
        CW = G[:, 1, 0:HALVES * 10 * NP].rearrange("p (h t n) -> p h t n", h=HALVES, n=NP)
        Whi = G[:, 1, 320:480].bitcast(F16).rearrange("p (h t n) -> p h t n", h=HALVES, n=NP)
        Wlo = G[:, 1, 480:640].bitcast(F16).rearrange("p (h t n) -> p h t n", h=HALVES, n=NP)

        conv_ps = ctx.enter_context(nc.psum_tensor("conv_ps", [P, 2, 2, 512], F32))
        out_ps = ctx.enter_context(nc.psum_tensor("out_ps", [P, 2, 512], F32))
        lg_ps = ctx.enter_context(nc.psum_tensor("lg_ps", [P, 512], F32))
        tr_ps = ctx.enter_context(nc.psum_tensor("tr_ps", [P, 512], F32))
        tr16 = tr_ps[:, :].bitcast(F16)
        means_ps = out_ps[:, 0, 0:2 * HALVES]
        pos_ps = [conv_ps[:, 1, 0, :], conv_ps[:, 1, 1, :], out_ps[:, 0, :]]

        small_in, weights_in, pos_in = sem("small_in"), sem("weights_in"), sem("pos_in")
        x_in = [[sem(f"x_in{k}{c}") for c in "ab"] for k in range(RING)]
        stored = [sem(f"stored{q}") for q in range(2 * STEPS)]
        pe_setup, vec_setup, act_setup, pool_setup = sem("pe_setup"), sem("vec_setup"), sem("act_setup"), sem("pool_setup")
        vec_step, pool_step = sem("vec_step"), sem("pool_step")
        conv_done, out_done = sem("conv_done"), sem("out_done")
        gelu_done = sem("gelu_done")
        out_added, y_done = sem("out_added"), sem("y_done")
        lg_done, lg_copied = sem("lg_done"), sem("lg_copied")
        t1_done, max_done, sub_done = sem("t1_done"), sem("max_done"), sem("sub_done")
        exp_done, soft_step, probs_ready = sem("exp_done"), sem("soft_step"), sem("probs_ready")
        t2_done, t2_copied = sem("t2_done"), sem("t2_copied")
        low_in = [[sem(f"low_in{k}{c}") for c in "ab"] for k in range(2)]
        sq_done = sem("sq_done")
        tot_done, group_done, group_copied = sem("tot_done"), sem("group_done"), sem("group_copied")
        norm_done = sem("norm_done")

        PE_KV, PE_A, PE_WT = 1, 2, 4
        PE_POS = (3, 5, 6)
        VEC_KV, VEC_A, VEC_WF, VEC_L0, VEC_WT, VEC_L1, VEC_L2 = range(1, 8)

        def until(eng, semaphore, value):
            if not isinstance(value, int) or value > 0:
                eng.wait_ge(semaphore, value)

        def halves(k):
            return ring[:, k * SL:(k + 1) * SL].rearrange("p (h y x) -> p h y x", h=HALVES, x=W)

        def place(j, u):
            r0, n, h = SPANS[u]
            return halves(j * BLOCKS + r0 // ROWS)[:, h, r0 % ROWS:r0 % ROWS + n, :].rearrange("p y x -> p (y x)")

        def passes(eng, body):
            body(0)
            with eng.Fori(1, PAIRS - 1) as i:
                body(i)
            body(PAIRS - 1)

        def late(k):
            return int(k % BLOCKS == 1)

        def fronted(t):
            return not isinstance(t, int) or t < LAST

        block = ctx.enter_context(nc.Block())

        @block.sync
        def _(sp):
            def unit(dram, b, u):
                r0, n, h = SPANS[u]
                return dram[b, h * P:(h + 1) * P, r0:r0 + n, :].rearrange("c y x -> c (y x)")

            def load(b, j, u):
                r0 = SPANS[u][0]
                arrived = x_in[j * BLOCKS + r0 // ROWS][r0 % ROWS // HROWS]
                sp.dma_start(place(j, u), unit(x, b, u)).then_inc(arrived, 16)

            sp.dma_start(par[:, :, :], params).then_inc(small_in, 16)
            sp.dma_start(pT[:, :, :], protoT.rearrange("(h p) n -> p h n", p=P)).then_inc(small_in, 16)
            for dst, src in ((kwS, kwT), (vwS, vwT), (qwS, qw), (owS, owT)):
                sp.dma_start(dst, src.rearrange("(h p) n -> p h n", p=P)).then_inc(weights_in, 16)
            sp.dma_start(dws[:, :, :], dw).then_inc(small_in, 16)
            sp.dma_start(idf[:, :], ident).then_inc(small_in, 16)
            sp.dma_start(gmat[:, :], group_mean).then_inc(small_in, 16)
            sp.dma_start(posS.rearrange("p h y x -> p h (y x)"), pos.rearrange("(h p) n -> p h n", p=P)).then_inc(pos_in, 16)
            for u in range(UNITS):
                load(0, 0, u)
            sp.wait_ge(vec_setup, VEC_L2)
            for u in range(UNITS):
                if u == 2:
                    sp.wait_ge(low_in[0][1], 48)
                if u >= 4 and u % 2 == 0:
                    sp.wait_ge(x_in[BLOCKS + (u - 4) // 4][u // 2 % 2], 32)
                load(1, 1, u)

            ORDER = [("store", 0, None), ("store", 1, None), ("load", 0, None), ("load", 1, None),
                     ("store", 2, ("load", 0)), ("store", 3, ("load", 1)), ("load", 2, None),
                     ("store", 4, ("store", 3)), ("load", 3, ("load", 2)),
                     ("store", 5, ("store", 4)), ("load", 4, ("load", 3)), ("load", 5, None)]
            assert STEPS == 6

            def store_and_reload(i, j, reload):
                def ended(what, q):
                    if what == "store":
                        until(sp, stored[j * STEPS + q], 32 * (i + 1))
                    else:
                        until(sp, x_in[j * BLOCKS + q // 2][q % 2], 32 * (i + 2))

                for what, q, after in ORDER:
                    for u in (2 * q, 2 * q + 1):
                        first = u % 2 == 0 and reload
                        if what == "store":
                            until(sp, norm_done, UNITS * (2 * i + j) + u + 1)
                        if after and first:
                            ended(*after)
                        if what == "store":
                            sp.dma_start(unit(out, 2 * i + j, u), place(j, u)).then_inc(stored[j * STEPS + q], 16)
                        elif reload:
                            if first:
                                ended("store", q)
                            load(2 * i + j + 2, j, u)

            store_and_reload(0, 0, True)
            with sp.Fori(1, PAIRS - 1) as i:
                store_and_reload(i - 1, 1, True)
                store_and_reload(i, 0, True)
            store_and_reload(PAIRS - 2, 1, True)
            store_and_reload(PAIRS - 1, 0, False)
            store_and_reload(PAIRS - 1, 1, False)
            for q in range(2 * STEPS):
                sp.wait_ge(stored[q], 32 * PAIRS)

        @block.gpsimd
        def _(pool):
            nc.gpsimd.memset(K32, 0.0)
            nc.gpsimd.memset(A32[:, :, :], 0.0)
            nc.gpsimd.memset(Wf, 0.0)
            nc.gpsimd.memset(neghalf[:, :], -0.5).then_inc(pool_setup, 1)
            nc.gpsimd.memset(Tlow[:, :, :], 0.0)
            nc.gpsimd.memset(Z[:, 0:2 * ZROW], 0.0)
            nc.gpsimd.memset(Z[:, (H + 2) * ZROW:(H + 3) * ZROW], 0.0)
            for k in range(2):
                nc.gpsimd.memset(T[:, k, :, 0:2], 0.0)
                nc.gpsimd.memset(T[:, k, :, TW - 2:TW], 0.0)
            pool.wait_ge(small_in, 80)
            nc.gpsimd.tensor_scalar(bnw[:, 0, :], par[:, BN_VAR, :], EPS, None, ALU.add).then_inc(pool_step, 1)
            pool.wait_ge(pool_step, 1)
            pool.wait_ge(pool_setup, 1)
            nc.gpsimd.tensor_tensor(bnw[:, 1, :], bnw[:, 0, :], neghalf[:, :], ALU.pow).then_inc(pool_step, 1)
            pool.wait_ge(pool_step, 2)
            nc.gpsimd.tensor_tensor(bnw[:, 2, :], bnw[:, 1, :], par[:, BN_G, :], ALU.mult).then_inc(pool_setup, 1)

            def normalise(b, j):
                until(pool, group_copied, b + 1)
                mean, msq = gst[:, 0, :], gst[:, 1, :]

                def step(inst):
                    pool.drain()

                step(nc.gpsimd.tensor_tensor(aff[:, 0, :], mean, mean, ALU.mult))
                step(nc.gpsimd.tensor_tensor(aff[:, 0, :], msq, aff[:, 0, :], ALU.subtract))
                step(nc.gpsimd.tensor_scalar(aff[:, 0, :], aff[:, 0, :], 0.0, EPS, ALU.max, ALU.add))
                step(nc.gpsimd.tensor_tensor(aff[:, 1, :], aff[:, 0, :], neghalf[:, :], ALU.pow))
                step(nc.gpsimd.tensor_tensor(aff[:, 2, :], aff[:, 1, :], par[:, GN_G, :], ALU.mult))
                step(nc.gpsimd.tensor_tensor(aff[:, 3, :], aff[:, 2, :], mean, ALU.mult))
                step(nc.gpsimd.tensor_tensor(aff[:, 4, :], par[:, GN_B, :], aff[:, 3, :], ALU.subtract))
                for u in range(UNITS):
                    h = SPANS[u][2]
                    at_u = place(j, u)
                    nc.gpsimd.tensor_scalar(at_u, at_u, aff[:, 2, h:h + 1], aff[:, 4, h:h + 1],
                                            ALU.mult, ALU.add).then_inc(norm_done, 1)

            normalise(0, 0)
            with pool.Fori(1, PAIRS - 1) as i:
                normalise(2 * i - 1, 1)
                normalise(2 * i, 0)
            for b in (B - 3, B - 2, B - 1):
                normalise(b, b % 2)

        @block.tensor
        def _(pe):
            small = conv_ps[:, 0, 0, :]
            pe.wait_ge(small_in, 80)
            pe.wait_ge(weights_in, 64)
            for n, w in enumerate((kwS, vwS)):
                for dh in range(HALVES):
                    for ch in range(HALVES):
                        last = nc.tensor.matmul(small[:, (2 * n + dh) * NP:(2 * n + dh + 1) * NP],
                                                w[:, ch, dh * P:(dh + 1) * P], pT[:, ch, :],
                                                start=ch == 0, stop=ch == HALVES - 1)
            last.then_inc(pe_setup, 1)
            pe.wait_ge(vec_setup, VEC_KV)
            second = conv_ps[:, 0, 1, :]
            for n, (w, r) in enumerate(((qwS, K32), (owS, vT))):
                for ch in range(HALVES):
                    for dh in range(HALVES):
                        nc.tensor.matmul(second[:, (2 * n + ch) * NP:(2 * n + ch + 1) * NP],
                                         w[:, dh, ch * P:(ch + 1) * P], r[:, dh, 0:NP],
                                         start=dh == 0, stop=dh == HALVES - 1)
            for dh in range(HALVES):
                last = nc.tensor.matmul(second[:, 64:65], K32[:, dh, :], par[:, Q_B, dh:dh + 1],
                                        start=dh == 0, stop=dh == HALVES - 1)
            last.then_inc(pe_setup, 1)
            TAPS = [[(0, 5 / 6), (-1, 1 / 6)], [(0, 1 / 2), (1, 1 / 2)], [(1, 5 / 6), (2, 1 / 6)]]
            SCALED = {1 / 6: 0, 5 / 6: 1, 1 / 2: 2}

            def resized_rows(kb, g, j):
                first = kb * ROWS + g * HROWS + j * (JROWS // 2)
                for phase in range(3):
                    ys = [y for y in range(first, first + JROWS // 2) if y % 3 == phase]
                    terms = [(ys, [min(max(2 * (y // 3) + d, 0), POS - 1) for y in ys], scale, ch)
                             for d, scale in TAPS[phase] for ch in range(HALVES)]
                    for n, (ys, src, scale, ch) in enumerate(terms):
                        step = src[1] - src[0] if len(src) > 1 else 1
                        yield (slice(ys[0] - first + g * 4, ys[-1] - first + g * 4 + 1, 3), slice(src[0], src[-1] + 1, step),
                               SCALED[scale], ch, n == 0, n == len(terms) - 1)

            pe.wait_ge(vec_setup, VEC_A)
            pe.wait_ge(pos_in, 16)

            def pos_logits(kb, halves_of_block):
                for g in halves_of_block:
                    for tiles in zip(*(resized_rows(kb, g, j) for j in range(JT))):
                        for j, (ys, src, scale, ch, first, final) in enumerate(tiles):
                            last = nc.tensor.matmul(
                                pos_ps[kb][32 * j:32 * j + 32, :].rearrange("p (y x) -> p y x", x=POS)[:, ys, :],
                                A3[:, scale, ch, :], posS[:, ch, src, :], start=first, stop=final)
                if g == 1:
                    last.then_inc(pe_setup, 1)

            pos_logits(0, (0, 1))
            pe.wait_ge(vec_setup, VEC_WF)
            for h in range(HALVES):
                turned = conv_ps[:, 0, h, :].bitcast(F16)
                for q in range(PASSES):
                    last = nc.tensor.transpose(turned[:, q * P:(q + 1) * P],
                                               Wf[:, h, q].rearrange("p s n -> p (s n)"), idh[:, :])
            last.then_inc(pe_setup, 1)

            def logits(m, pair, k, g):
                until(pe, x_in[k][g], 32 * (pair + 1))
                until(pe, sub_done, 2 * m + g)
                xs = halves(k)
                for ch in range(HALVES):
                    for j in range(JT):
                        r0 = g * HROWS + j * (JROWS // 2)
                        last = nc.tensor.matmul(lg_ps[32 * j:32 * j + 32, 0:JROWS // 2 * W], A32[:, ch, 0:32],
                                                xs[:, ch, r0:r0 + JROWS // 2, :],
                                                start=ch == 0, stop=ch == HALVES - 1)
                last.then_inc(lg_done, 1)

            def turn_logits(m, g):
                until(pe, lg_copied, 2 * m + g + 1)
                for i in range(JROWS // 2):
                    last = nc.tensor.transpose(lg_ps[0:W, i * P:(i + 1) * P], Ls[:, i * W:(i + 1) * W], idf[:, :])
                last.then_inc(t1_done, 1)

            def turn_probs(t, kb, g):
                if g == T2G - 1 and kb < BLOCKS - 1:
                    until(pe, probs_ready, t + 2)
                elif g == 0:
                    until(pe, probs_ready, t + 1)
                until(pe, t2_copied, T2G * t + g)
                first, rows = GROUPS[g]
                for r in range(rows):
                    at = (kb * ROWS + first + r + 1) * ZROW + NP
                    last = nc.tensor.transpose(tr16[:, r * W:(r + 1) * W], Z[:, at:at + P], idh[0:W, 0:W])
                last.then_inc(t2_done, 1)

            def group_means(b):
                until(pe, tot_done, b + 1)
                nc.tensor.matmul(means_ps, gmat[:, :], tot[:, :, :].rearrange("p a h -> p (a h)"),
                                 start=True, stop=True).then_inc(group_done, 1)

            def conv_half(i, k, n, row_half):
                h, s = divmod(n, STRIPS)
                y0 = row_half * HROWS
                for dx in range(3):
                    nc.tensor.matmul(conv_ps[:, n % 2, row_half, :], Wt[:, h * PASSES + dx, :],
                                     T[:, k % 2, 1 + y0:1 + y0 + HROWS, 1 + s * COLS + dx:1 + s * COLS + dx + COLS],
                                     start=dx == 0, stop=False)
                if n == 0:
                    until(pe, low_in[k % 2][row_half], 48 * (RING // 2 * i + k // 2 + 1))
                shifted = Tlow[:, k % 2, :].rearrange("p (y x) -> p y x", x=TW)
                return nc.tensor.matmul(conv_ps[:, n % 2, row_half, :], Wt[:, h * PASSES + LOW, :],
                                        shifted[:, y0:y0 + HROWS, 1 + s * COLS:1 + s * COLS + COLS],
                                        start=False, stop=True)

            for m in range(2):
                for g in range(2):
                    logits(m, 0, m, g)
                    pos_logits(m + 1, (g,))
                    turn_logits(m, g)
            pe.wait_ge(vec_setup, VEC_WT)
            pe.wait_ge(act_setup, BLOCKS)
            pe.wait_ge(pool_setup, 2)
            for g in range(T2G - 1):
                turn_probs(0, 0, g)

            def body(i):
                for k in range(RING):
                    t, kb, m, mk = RING * i + k, k % BLOCKS, RING * i + k + 2, (k + 2) % RING
                    image_ended = kb == 0 and not (isinstance(t, int) and t == 0)
                    for n in range(TILES):
                        h, s = divmod(n, STRIPS)
                        at = TILES * t + n
                        if n == 0:
                            until(pe, t2_copied, T2G * t + 2)
                        if n != 1:
                            until(pe, gelu_done, at - 1)
                            conv_half(i, k, n, 0)
                        if n == 0:
                            if fronted(m) and not late(k):
                                logits(m, i + (k + 2) // RING, mk, 0)
                            turn_probs(t, kb, T2G - 1)
                            until(pe, gelu_done, at)
                            conv_half(i, k, 1, 0)
                            if fronted(t + 1):
                                turn_probs(t + 1, (k + 1) % BLOCKS, 0)
                            until(pe, t2_copied, T2G * (t + 1))
                        if n == 1 and fronted(m) and late(k):
                            logits(m, i + (k + 2) // RING, mk, 0)
                        if n == 2 + late(k) and fronted(m):
                            turn_logits(m, 1)
                        conv_half(i, k, n, 1).then_inc(conv_done, 1)
                        until(pe, out_added, at)
                        if n == 1 and image_ended:
                            group_means(2 * i + k // BLOCKS - 1)
                            until(pe, group_copied, 2 * i + k // BLOCKS)
                        for row_half in range(2):
                            last = nc.tensor.matmul(
                                out_ps[:, row_half, :], Wt[:, h * PASSES + PLAIN, :],
                                T[:, k % 2, 1 + row_half * HROWS:1 + (row_half + 1) * HROWS, 2 + s * COLS:2 + s * COLS + COLS],
                                start=True, stop=True)
                        last.then_inc(out_done, 1)
                        if n == late(k) and fronted(m):
                            turn_logits(m, 0)
                        if n == 1 + late(k) and fronted(m):
                            logits(m, i + (k + 2) // RING, mk, 1)
                        if n < 3 and fronted(t + 1):
                            turn_probs(t + 1, (k + 1) % BLOCKS, n + 1)

            passes(pe, body)
            pe.wait_ge(out_added, TILES * LAST)
            group_means(B - 1)

        @block.scalar
        def _(act):
            act.wait_ge(vec_setup, VEC_A)

            def take_pos(kb):
                act.wait_ge(pe_setup, PE_POS[kb])
                nc.scalar.activation(narrow[:, kb].rearrange("p y x -> p (y x)"), pos_ps[kb], ACT.Identity,
                                     bias=l0c[:, :]).then_inc(act_setup, 1)

            take_pos(0)
            take_pos(1)
            act.wait_ge(vec_setup, VEC_WT)
            act.wait_ge(pool_setup, 2)

            def exponent(m):
                act.wait_ge(sub_done, 2 * m + 2)
                nc.scalar.activation(E[:, :, :], E[:, :, :], ACT.Exp).then_inc(exp_done, 1)

            def copy_probs(t, buf, g):
                if g == 0:
                    until(act, out_done, TILES * (t - 1))
                act.wait_ge(t2_done, T2G * t + g + 1)
                first, rows = GROUPS[g]
                nc.scalar.activation(T[:, buf, first + 1:first + 1 + rows, 2:2 + W],
                                     tr16[:, 0:rows * W].rearrange("p (y x) -> p y x", x=W), ACT.Copy)\
                    .then_inc(t2_copied, 1)

            def shift_probs(t, buf, part):
                act.wait_ge(t2_copied, T2G * t + 2 * (part + 1))
                flat = T[2 * NP:3 * NP, buf, :, :].rearrange("p y x -> p (y x)")
                n = HROWS * TW
                for dx in range(3):
                    act.dma_start(Tlow[dx * NP:(dx + 1) * NP, buf, part * n:(part + 1) * n],
                                  flat[:, part * n + dx:(part + 1) * n + dx]).then_inc(low_in[buf][part], 16)

            def square(k, n, at):
                h, s = divmod(n, STRIPS)
                act.wait_ge(y_done, at + 1)
                until(act, sq_done, at)
                c = (k % BLOCKS) * STRIPS + s
                nc.scalar.activation(junk[:, :].rearrange("p (y x) -> p y x", x=COLS),
                                     halves(k)[:, h, :, s * COLS:(s + 1) * COLS], ACT.Square,
                                     accum_out=ystat[:, 1, h, c:c + 1]).then_inc(sq_done, 1)

            SQUARES = [{3: (0,), 4: (1,), 5: (2,)},
                       {0: (-3,), 1: (-2,), 2: (-1, 0), 4: (1,), 5: (2,)},
                       {0: (-3,), 1: (-2, -1), 3: (0,), 4: (1, 2), 5: (3,)}]

            def squares(k, t, tiles):
                for n in tiles:
                    if n >= 0 or not (isinstance(t, int) and t == 0):
                        square((k - (n < 0)) % RING, n % TILES, TILES * t + n)

            exponent(0)
            take_pos(2)
            exponent(1)
            for g in range(T2G - 1):
                copy_probs(0, 0, g)
                if g in (1, 3):
                    shift_probs(0, 0, g // 2)

            def body(i):
                for k in range(RING):
                    t = RING * i + k
                    image_ended = k % BLOCKS == 0 and not (isinstance(t, int) and t == 0)
                    for n in range(TILES):
                        h = n // STRIPS
                        at = TILES * t + n
                        if n == 0:
                            copy_probs(t, k % 2, T2G - 1)
                        if n < T2G - 1 and fronted(t + 1):
                            copy_probs(t + 1, (k + 1) % 2, n)
                        if n == 0 and image_ended:
                            squares(k, t, (-2, -1))
                        act.wait_ge(conv_done, at + 1)
                        until(act, y_done, at - 1)
                        nc.scalar.activation(G[:, n % 2, :], conv_ps[:, n % 2, :, :].rearrange("p a b -> p (a b)"),
                                             ACT.Gelu, bias=gb[:, h:h + 1], scale=gs[:, h:h + 1])\
                            .then_inc(gelu_done, 1)
                        if n in (1, 3) and fronted(t + 1):
                            shift_probs(t + 1, (k + 1) % 2, n // 2)
                        if n == 2 + late(k) and fronted(t + 2):
                            exponent(t + 2)
                            nc.scalar.activation(warm[:, :], neghalf[:, :], ACT.Gelu)
                        squares(k, t, SQUARES[k % BLOCKS].get(n, ()))

            passes(act, body)
            for n in (4, 5):
                square(RING - 1, n, TILES * (LAST - 1) + n)

        @block.vector
        def _(dve):
            count = [0]

            def step(inst):
                count[0] += 1
                inst.then_inc(vec_step, 1)
                dve.wait_ge(vec_step, count[0])

            small = conv_ps[:, 0, 0, :]
            second = conv_ps[:, 0, 1, :]
            dve.wait_ge(small_in, 80)
            dve.wait_ge(pool_setup, 1)
            nc.vector.tensor_copy(idh[:, :], idf[:, :])
            dve.wait_ge(pe_setup, PE_KV)
            for dh in range(HALVES):
                nc.vector.tensor_scalar(K32[:, dh, :].rearrange("p (j n) -> p j n", n=32)[:, :, 0:NP],
                                        small[:, dh * NP:(dh + 1) * NP].unsqueeze(1).to_broadcast([P, JT, NP]),
                                        par[:, K_B, dh:dh + 1], C ** -0.5, ALU.add, ALU.mult)
                last = nc.vector.tensor_scalar(vT[:, dh, :], small[:, (2 + dh) * NP:(3 + dh) * NP],
                                               par[:, V_B, dh:dh + 1], None, ALU.add)
            last.then_inc(vec_setup, 1)
            dve.wait_ge(pe_setup, PE_A)
            nc.vector.tensor_copy(l0c[:, :], second[:, 64:65])
            made = second[:, 0:HALVES * NP].rearrange("p (h n) -> p h n", h=HALVES)
            step(nc.vector.tensor_copy(A32[:, :, 0:NP], made))
            for n, scale in enumerate((1 / 6, 5 / 6, 1 / 2)):
                last = nc.vector.tensor_scalar(A3[:, n], A32[:, :, :], scale, None, ALU.mult)
            last.then_inc(vec_setup, 1)

            for h in range(HALVES):
                last = nc.vector.tensor_scalar(CW[:, h, 9, :], second[:, (2 + h) * NP:(3 + h) * NP],
                                               par[:, OUT_B, h:h + 1], None, ALU.add)
            step(last)
            for h in range(HALVES):
                last = nc.vector.tensor_tensor(CW[:, h, 0:9, :], CW[:, h, 9:10, :].to_broadcast([P, 9, NP]),
                                               dws[:, h, :].unsqueeze(2).to_broadcast([P, 9, NP]), ALU.mult)
            step(last)
            nc.vector.tensor_reduce(mag[:, 0, :], CW[:, :, 0:9, :].rearrange("p h t n -> p h (t n)"), AX, ALU.max,
                                    apply_absolute_value=True)
            step(nc.vector.tensor_reduce(mag[:, 1, :], CW[:, :, 9, :], AX, ALU.max, apply_absolute_value=True))
            step(nc.vector.tensor_scalar(mag[:, 0:2, :], mag[:, 0:2, :], 1e-30, None, ALU.max))
            step(nc.vector.tensor_scalar(mag[:, 0:2, :].bitcast(I32), mag[:, 0:2, :].bitcast(I32), 0x7F800000, None,
                                         ALU.bitwise_and))
            step(nc.vector.reciprocal(mag[:, 2:4, :], mag[:, 0:2, :]))
            for h in range(HALVES):
                nc.vector.tensor_scalar(CW[:, h, 0:9, :], CW[:, h, 0:9, :], mag[:, 2, h:h + 1], WT_SCALE,
                                        ALU.mult, ALU.mult)
                last = nc.vector.tensor_scalar(CW[:, h, 9, :], CW[:, h, 9, :], mag[:, 3, h:h + 1], WT_SCALE,
                                               ALU.mult, ALU.mult)
            step(last)
            step(nc.vector.tensor_copy(Whi, CW))
            step(nc.vector.tensor_tensor(Wlo, CW, Whi, ALU.subtract))
            for h in range(HALVES):
                def fill(slot, count, src, taps, q=slice(0, 3)):
                    shape = [P, q.stop - q.start, count, NP]
                    return nc.vector.tensor_copy(Wf[:, h, q, slot:slot + count, :],
                                                 src[:, h, taps, :].unsqueeze(2).to_broadcast(shape))
                fill(0, 2, Whi, slice(0, 3))
                fill(2, 2, Whi, slice(3, 6))
                fill(4, 1, Wlo, slice(3, 6))
                fill(5, 2, Whi, slice(6, 9))
                fill(7, 1, Wlo, slice(6, 9))
                nc.vector.tensor_copy(Wf[:, h, LOW, 0:3, :], Wlo[:, h, 0:3, :])
                fill(2, 2, Whi, slice(9, 10), slice(PLAIN, PLAIN + 1))
                last = fill(4, 1, Wlo, slice(9, 10), slice(PLAIN, PLAIN + 1))
            last.then_inc(vec_setup, 1)
            dve.wait_ge(pool_setup, 2)
            step(nc.vector.tensor_tensor(gb[:, :], par[:, BN_MEAN, :], bnw[:, 2, :], ALU.mult))
            nc.vector.tensor_tensor(gb[:, :], par[:, BN_B, :], gb[:, :], ALU.subtract)
            step(nc.vector.tensor_tensor(gs[:, :], mag[:, 0, :], bnw[:, 2, :], ALU.mult))
            nc.vector.tensor_scalar(gs[:, :], gs[:, :], UNSCALE, None, ALU.mult)
            nc.vector.tensor_scalar(osc[:, :], mag[:, 1, :], UNSCALE, None, ALU.mult)
            def mix(o, whole, part, by):
                return nc.vector.scalar_tensor_tensor(out=o, in0=whole, scalar=by, in1=part, op0=ALU.mult, op1=ALU.add)

            def resize_columns(kb):
                src, dst = narrow[:, kb], L0[:, kb, :].rearrange("p (y x) -> p y x", x=W)
                dve.wait_ge(act_setup, kb + 1)
                nc.vector.tensor_copy(dst[:, :, 0:1], src[:, :, 0:1])
                nc.vector.tensor_copy(dst[:, :, W - 1:W], src[:, :, POS - 1:POS])
                step(nc.vector.tensor_scalar(sixth, src, 1 / 6, None, ALU.mult))
                step(nc.vector.tensor_scalar(half, src[:, :, 1::2], 1 / 2, None, ALU.mult))
                mix(dst[:, :, 3::3], src[:, :, 2::2], sixth[:, :, 1:POS - 1:2], 5 / 6)
                mix(dst[:, :, 1::3], src[:, :, 0::2], half, 1 / 2)
                mix(dst[:, :, 2:W - 1:3], src[:, :, 1:POS - 1:2], sixth[:, :, 2::2], 5 / 6).then_inc(vec_setup, 1)

            resize_columns(0)
            dve.wait_ge(vec_setup, VEC_L0)
            dve.wait_ge(pe_setup, PE_WT)
            for h in range(HALVES):
                last = nc.vector.tensor_copy(Wt[:, h * PASSES:(h + 1) * PASSES, :].rearrange("p q c -> p (q c)"),
                                             conv_ps[:, 0, h, :].bitcast(F16)[:, 0:PASSES * P])
            last.then_inc(vec_setup, 1)


            HALF = JROWS // 2 * W

            def add_l0(m, kb, g):
                dve.wait_ge(lg_done, 2 * m + g + 1)
                until(dve, t1_done, 2 * m + g)
                nc.vector.tensor_tensor(Ls[:, :], lg_ps[:, 0:HALF],
                                        L0[:, kb, g * HALF:(g + 1) * HALF], ALU.add).then_inc(lg_copied, 1)

            def subtract_max(m, g):
                dve.wait_ge(t1_done, 2 * m + g + 1)
                lg = lg_ps[0:W, :].rearrange("x (i j n) -> x i j n", i=JROWS // 2, n=32)[:, :, :, 0:NP]
                most = mx[:, g * 16:(g + 1) * 16].rearrange("x (i j) -> x i j", j=JT)
                nc.vector.tensor_reduce(most, lg, AX, ALU.max).then_inc(max_done, 1)
                dve.wait_ge(max_done, 2 * m + g + 1)
                dst = E[:, g * HROWS:(g + 1) * HROWS, :].rearrange("x (j i) n -> x i j n", j=JT)
                nc.vector.tensor_tensor(dst, lg, most.unsqueeze(3).to_broadcast([W, JROWS // 2, JT, NP]),
                                        ALU.subtract).then_inc(sub_done, 1)

            SOFT = 5

            def sum_exp(m):
                dve.wait_ge(exp_done, m + 1)
                nc.vector.tensor_reduce(rs[:, 0, :], E[:, :, :], AX, ALU.add).then_inc(soft_step, 1)

            def invert_sum(m):
                dve.wait_ge(soft_step, SOFT * m + 1)
                nc.vector.reciprocal(rs[:, 1, :], rs[:, 0, :]).then_inc(soft_step, 1)

            def scale_exp(m):
                dve.wait_ge(soft_step, SOFT * m + 2)
                nc.vector.scalar_tensor_tensor(out=E[:, :, :], in0=E[:, :, :], scalar=PROB_SCALE,
                                               in1=rs[:, 1, :].unsqueeze(2).to_broadcast([W, ROWS, NP]),
                                               op0=ALU.mult, op1=ALU.mult).then_inc(soft_step, 1)

            def z_rows(kb):
                r0 = 2 + kb * ROWS
                return Z[:, r0 * ZROW:(r0 + ROWS) * ZROW].rearrange("x (y c n) -> x y c n", c=3, n=NP)

            def high_probs(m, kb):
                until(dve, t2_done, T2G * (m - 2) + 1)
                dve.wait_ge(soft_step, SOFT * m + 3)
                nc.vector.tensor_copy(z_rows(kb)[:, :, 0, :], E[:, :, :]).then_inc(soft_step, 1)

            def low_probs(m, kb):
                dve.wait_ge(soft_step, SOFT * m + 4)
                z = z_rows(kb)
                nc.vector.tensor_tensor(z[:, :, 1, :], E[:, :, :], z[:, :, 0, :], ALU.subtract).then_inc(soft_step, 1)

            def high_again(m, kb):
                dve.wait_ge(soft_step, SOFT * m + 5)
                z = z_rows(kb)
                nc.vector.tensor_copy(z[:, :, 2, :], z[:, :, 0, :]).then_inc(probs_ready, 1)

            def add_out(k, n, at):
                h, s = divmod(n, STRIPS)
                dve.wait_ge(out_done, at + 1)
                v = halves(k)[:, h, :, s * COLS:(s + 1) * COLS]
                nc.vector.scalar_tensor_tensor(out=v, in0=out_ps[:, :, :].rearrange("p a (y x) -> p (a y) x", x=COLS),
                                               scalar=osc[:, h:h + 1], in1=v, op0=ALU.mult, op1=ALU.add)\
                    .then_inc(out_added, 1)

            def add_gelu(k, n, at):
                h, s = divmod(n, STRIPS)
                dve.wait_ge(gelu_done, at + 1)
                dve.wait_ge(out_added, at + 1)
                v = halves(k)[:, h, :, s * COLS:(s + 1) * COLS]
                c = (k % BLOCKS) * STRIPS + s
                nc.vector.scalar_tensor_tensor(out=v, in0=G[:, n % 2, :].rearrange("p (y x) -> p y x", x=COLS), scalar=1.0,
                                               in1=v, op0=ALU.mult, op1=ALU.add, accum_out=ystat[:, 0, h, c:c + 1])\
                    .then_inc(y_done, 1)

            def sum_image(t, b):
                dve.wait_ge(sq_done, TILES * t)
                dve.wait_ge(y_done, TILES * t)
                nc.vector.tensor_reduce(tot[:, :, :], ystat[:, :, :, :], AX, ALU.add).then_inc(tot_done, 1)
                dve.wait_ge(tot_done, b + 1)

            def take_means(b):
                dve.wait_ge(group_done, b + 1)
                until(dve, norm_done, UNITS * (b - 1) + 1)
                nc.vector.tensor_copy(gst[:, :, :].rearrange("p a h -> p (a h)"), means_ps)\
                    .then_inc(group_copied, 1)

            def probabilities(m):
                sum_exp(m)
                invert_sum(m)
                scale_exp(m)
                high_probs(m, m)
                low_probs(m, m)
                high_again(m, m)

            for g in range(2):
                add_l0(0, 0, g)
                subtract_max(0, g)
            resize_columns(1)
            dve.wait_ge(vec_setup, VEC_L1)
            add_l0(1, 1, 0)
            probabilities(0)
            subtract_max(1, 0)
            add_l0(1, 1, 1)
            subtract_max(1, 1)
            probabilities(1)
            resize_columns(2)
            dve.wait_ge(vec_setup, VEC_L2)

            def body(i):
                for k in range(RING):
                    t, m = RING * i + k, RING * i + k + 2
                    mb = (k + 2) % BLOCKS
                    b = 2 * i + k // BLOCKS - 1
                    image_ended = k % BLOCKS == 0 and not (isinstance(t, int) and t == 0)
                    for n in range(TILES):
                        at = TILES * t + n
                        front = fronted(m)
                        phase = n - late(k) if front else -1
                        if n == 0:
                            if not (isinstance(t, int) and t == 0):
                                add_gelu((k - 1) % RING, TILES - 1, at - 1)
                            if phase == 0:
                                add_l0(m, mb, 0)
                            add_out(k, n, at)
                            continue
                        if phase == 0:
                            add_l0(m, mb, 0)
                        if phase == 1:
                            subtract_max(m, 0)
                        if n == 1 and image_ended:
                            sum_image(t, b)
                            take_means(b)
                        if phase == 2:
                            add_l0(m, mb, 1)
                            subtract_max(m, 1)
                        if phase == 3 and not late(k):
                            sum_exp(m)
                        add_out(k, n, at)
                        if phase == 3:
                            if late(k):
                                sum_exp(m)
                            invert_sum(m)
                            scale_exp(m)
                            high_probs(m, mb)
                        add_gelu(k, n - 1, at - 1)
                        if phase == 3:
                            low_probs(m, mb)
                            high_again(m, mb)

            passes(dve, body)
            add_gelu(RING - 1, TILES - 1, TILES * LAST - 1)
            sum_image(LAST, B - 1)
            take_means(B - 1)


def kernel(**inputs):
    import concourse.bacc as bacc
    from concourse.bass_utils import run_bass_kernel_spmd

    a = {k.removeprefix("L0_conv_"): np.asarray(v) for k, v in inputs.items()}
    vectors = np.stack([a[n] for n in ("q_b", "k_b", "v_b", "out_b", "bn_g", "bn_b", "bn_mean", "bn_var", "gn_g", "gn_b")])
    same_group = np.kron(np.eye(P // GROUP), np.ones((GROUP, GROUP)))
    arrays = {
        "x": a["x"],
        "params": vectors.reshape(10, HALVES, P).transpose(2, 0, 1),
        "dw": a["dw_w"].reshape(HALVES, P, 9).transpose(1, 0, 2),
        "qw": a["q_w"],
        "kwT": a["k_w"].T,
        "vwT": a["v_w"].T,
        "owT": a["out_w"].T,
        "protoT": a["prototypes"][0].T,
        "pos": a["pos_embed"].reshape(C, POS * POS),
        "ident": np.eye(P, dtype=np.float32),
        "group_mean": (same_group / (GROUP * H * W)).astype(np.float32),
    }
    arrays = {f"in_{k}": np.ascontiguousarray(v) for k, v in arrays.items()}
    nc = bacc.Bacc("TRN2", target_bir_lowering=False, num_devices=1)
    args = [nc.dram_tensor(k, v.shape, mybir.dt.from_np(v.dtype), kind="ExternalInput").ap() for k, v in arrays.items()]
    out = nc.dram_tensor("out", (B, C, H, W), F32, kind="ExternalOutput").ap()
    build(nc, *args, out)
    r = run_bass_kernel_spmd(nc, [arrays], core_ids=[0])
    return r.results[0]["out"]
```
